# Optimizing a Trainium2 kernel written in Bass

```python
import numpy as np
import jax
import jax.numpy as jnp

def _softmax(x, axis=-1):
    return jax.nn.softmax(x, axis=axis)

def _gelu(x):
    return jax.nn.gelu(x, approximate=True)

def _silu(x):
    return jax.nn.silu(x)

def _sigmoid(x):
    return jax.nn.sigmoid(x)

def _layernorm(x, axis=-1, eps=1e-05):
    m = jnp.mean(x, axis=axis, keepdims=True)
    v = jnp.var(x, axis=axis, keepdims=True)
    return (x - m) / jnp.sqrt(v + eps)

def _scatter_add(tgt, idx, src, axis=0):
    return tgt.at[idx].add(src)

def _segment_sum(src, seg, n):
    return jax.ops.segment_sum(src, seg, n)
kernel_name = 'mk_decoder_postln_d1_seqx_r4_e75f2b'

def setup_inputs(seed: int=0):
    np.random.seed(seed)
    _w = jnp.asarray

    def _rec_inputs():
        import jax
        import jax.numpy as jnp
        _rk = jax.random.key(seed)
        x = 0.0002417 + 0.9998 * jax.random.normal(jax.random.fold_in(_rk, 1), (8, 256, 256), jnp.float32)
        _lenS = 256 - jax.random.randint(jax.random.fold_in(_rk, 7), (8,), 0, max(1, 256 // 4) + 1, jnp.int32)
        _lenS2 = 256 - jax.random.randint(jax.random.fold_in(_rk, 8), (8,), 0, max(1, 256 // 4) + 1, jnp.int32)
        _ctx_1024P = jax.random.normal(jax.random.fold_in(_rk, 11), (8, 16, 256), jnp.float32)
        _ctx_1024c = jax.random.dirichlet(jax.random.fold_in(_rk, 511), 0.3 * jnp.ones((16,), jnp.float32), (8, 256))
        _ctx_1024t = jnp.einsum('bsk,bkd->bsd', _ctx_1024c, _ctx_1024P)
        _ctx_1024t = _ctx_1024t * jax.lax.rsqrt(jnp.mean(jnp.square(_ctx_1024t)) + 1e-12) * 0.953939
        ctx_1024 = 7.22013e-05 + 1.00017 * (_ctx_1024t + 0.3 * jax.random.normal(jax.random.fold_in(_rk, 611), (8, 256, 256), jnp.float32))
        return (x, ctx_1024)
    x, ctx_1024 = _rec_inputs()

    def _L0_attn_setup():
        import jax, jax.numpy as jnp
        import numpy as np
        D_MODEL = 256
        N_LAYERS = 2
        D_STATE = 64
        D_CONV = 4
        EXPAND = 2
        D_INNER = EXPAND * D_MODEL
        DT_RANK = (D_MODEL + 15) // 16
        BATCH, SEQLEN = (2, 256)

        def _silu(x):
            return x * jax.nn.sigmoid(x)

        def _causal_dwconv(x, w, b):
            K = w.shape[-1]
            L = x.shape[1]
            xp = jnp.pad(x, ((0, 0), (K - 1, 0), (0, 0)))
            y = sum((xp[:, k:k + L, :] * w[:, k] for k in range(K)))
            return y + b

        def _selective_scan(u, dt, A, Bm, C, D_skip):
            B, L, dI = u.shape
            dS = A.shape[-1]

            def step(h, inp):
                u_t, dt_t, B_t, C_t = inp
                dA = jnp.exp(dt_t[:, :, None] * A)
                h = h * dA + (dt_t * u_t)[:, :, None] * B_t[:, None, :]
                y = jnp.einsum('bds,bs->bd', h, C_t)
                return (h, y)
            h0 = jnp.zeros((B, dI, dS), u.dtype)
            xs = (u.transpose(1, 0, 2), dt.transpose(1, 0, 2), Bm.transpose(1, 0, 2), C.transpose(1, 0, 2))
            _, ys = jax.lax.scan(step, h0, xs)
            return ys.transpose(1, 0, 2) + u * D_skip

        def _mamba_block(x, in_w, cw, cb, xp_w, dtw, dtb, A_log, D_skip, out_w):
            xz = jnp.einsum('bld,ed->ble', x, in_w)
            u, z = jnp.split(xz, 2, axis=-1)
            u = _silu(_causal_dwconv(u, cw, cb))
            x_dbl = jnp.einsum('bld,ed->ble', u, xp_w)
            dt, Bm, C = jnp.split(x_dbl, [DT_RANK, DT_RANK + D_STATE], axis=-1)
            dt = jax.nn.softplus(jnp.einsum('blr,dr->bld', dt, dtw) + dtb)
            A = -jnp.exp(A_log)
            y = _selective_scan(u, dt, A, Bm, C, D_skip)
            y = y * _silu(z)
            return jnp.einsum('bld,ed->ble', y, out_w)
        key = jax.random.key(seed)
        ks = jax.random.split(key, 8)
        n = lambda i, shape, scale: jax.random.normal(ks[i], shape, jnp.float32) * scale
        A_log = jnp.log(jnp.tile(jnp.arange(1, D_STATE + 1, dtype=jnp.float32)[None, None, :], (N_LAYERS, D_INNER, 1)))
        return {'x': n(0, (BATCH, SEQLEN, D_MODEL), 1.0), 'in_proj_w': n(1, (N_LAYERS, 2 * D_INNER, D_MODEL), 0.02), 'conv_w': n(2, (N_LAYERS, D_INNER, D_CONV), 0.2), 'conv_b': jnp.zeros((N_LAYERS, D_INNER), jnp.float32), 'x_proj_w': n(3, (N_LAYERS, DT_RANK + 2 * D_STATE, D_INNER), 0.02), 'dt_proj_w': n(4, (N_LAYERS, D_INNER, DT_RANK), 0.02), 'dt_proj_b': n(5, (N_LAYERS, D_INNER), 0.1), 'A_log': A_log, 'D_skip': jnp.ones((N_LAYERS, D_INNER), jnp.float32), 'out_proj_w': n(6, (N_LAYERS, D_MODEL, D_INNER), 0.02)}
    _L0_attn_all = _L0_attn_setup()
    _L0_attn_in = {k: v for k, v in _L0_attn_all.items() if k in ('in_proj_w', 'conv_w', 'conv_b', 'x_proj_w', 'dt_proj_w', 'dt_proj_b', 'A_log', 'D_skip', 'out_proj_w')}
    del _L0_attn_all

    def _L0_xattn_setup():
        import jax, jax.numpy as jnp
        import numpy as np
        D_MODEL = 256
        B, S = (4, 512)
        key = jax.random.key(seed)
        ks = jax.random.split(key, 10)
        s = 1.0 / np.sqrt(D_MODEL)
        return {'k': jax.random.normal(ks[0], (B, S, D_MODEL), jnp.float32), 'v': jax.random.normal(ks[1], (B, S, D_MODEL), jnp.float32), 'q': jax.random.normal(ks[2], (B, S, D_MODEL), jnp.float32), 'Wk': jax.random.normal(ks[3], (D_MODEL, D_MODEL), jnp.float32) * s, 'Wv': jax.random.normal(ks[4], (D_MODEL, D_MODEL), jnp.float32) * s, 'bv': jnp.zeros((D_MODEL,), jnp.float32), 'Wq': jax.random.normal(ks[5], (D_MODEL, D_MODEL), jnp.float32) * s, 'bq': jnp.zeros((D_MODEL,), jnp.float32), 'Wo': jax.random.normal(ks[6], (D_MODEL, D_MODEL), jnp.float32) * s, 'bo': jnp.zeros((D_MODEL,), jnp.float32)}
    _L0_xattn_all = _L0_xattn_setup()
    _L0_xattn_in = {k: v for k, v in _L0_xattn_all.items() if k in ('Wk', 'Wv', 'bv', 'Wq', 'bq', 'Wo', 'bo')}
    del _L0_xattn_all

    def _L0_ffn_setup():
        import jax, jax.numpy as jnp
        import numpy as np
        D_MODEL = 256
        NUM_EXPERTS = 8
        HIDDEN = 1024
        TOP_K = 2
        key = jax.random.key(seed)
        ks = jax.random.split(key, 6)
        x = jax.random.normal(ks[0], (2, 256, D_MODEL), dtype=jnp.float32)
        gate_w = jax.random.normal(ks[1], (NUM_EXPERTS, D_MODEL), dtype=jnp.float32) * (1.0 / np.sqrt(D_MODEL))
        w1 = jax.random.normal(ks[2], (NUM_EXPERTS, HIDDEN, D_MODEL), dtype=jnp.float32) * (1.0 / np.sqrt(D_MODEL))
        b1 = jax.random.normal(ks[3], (NUM_EXPERTS, HIDDEN), dtype=jnp.float32) * 0.01
        w2 = jax.random.normal(ks[4], (NUM_EXPERTS, D_MODEL, HIDDEN), dtype=jnp.float32) * (1.0 / np.sqrt(HIDDEN))
        b2 = jax.random.normal(ks[5], (NUM_EXPERTS, D_MODEL), dtype=jnp.float32) * 0.01
        return {'x': x, 'gate_w': gate_w, 'w1': w1, 'b1': b1, 'w2': w2, 'b2': b2}
    _L0_ffn_all = _L0_ffn_setup()
    _L0_ffn_in = {k: v for k, v in _L0_ffn_all.items() if k in ('gate_w', 'w1', 'b1', 'w2', 'b2')}
    del _L0_ffn_all
    return {'x': x, 'ctx_1024': ctx_1024, 'L0_attn_in_proj_w': _L0_attn_in['in_proj_w'], 'L0_attn_conv_w': _L0_attn_in['conv_w'], 'L0_attn_conv_b': _L0_attn_in['conv_b'], 'L0_attn_x_proj_w': _L0_attn_in['x_proj_w'], 'L0_attn_dt_proj_w': _L0_attn_in['dt_proj_w'], 'L0_attn_dt_proj_b': _L0_attn_in['dt_proj_b'], 'L0_attn_A_log': _L0_attn_in['A_log'], 'L0_attn_D_skip': _L0_attn_in['D_skip'], 'L0_attn_out_proj_w': _L0_attn_in['out_proj_w'], 'L0_xattn_Wk': _L0_xattn_in['Wk'], 'L0_xattn_Wv': _L0_xattn_in['Wv'], 'L0_xattn_bv': _L0_xattn_in['bv'], 'L0_xattn_Wq': _L0_xattn_in['Wq'], 'L0_xattn_bq': _L0_xattn_in['bq'], 'L0_xattn_Wo': _L0_xattn_in['Wo'], 'L0_xattn_bo': _L0_xattn_in['bo'], 'L0_ffn_gate_w': _L0_ffn_in['gate_w'], 'L0_ffn_w1': _L0_ffn_in['w1'], 'L0_ffn_b1': _L0_ffn_in['b1'], 'L0_ffn_w2': _L0_ffn_in['w2'], 'L0_ffn_b2': _L0_ffn_in['b2']}

def reference(x, ctx_1024, L0_attn_in_proj_w, L0_attn_conv_w, L0_attn_conv_b, L0_attn_x_proj_w, L0_attn_dt_proj_w, L0_attn_dt_proj_b, L0_attn_A_log, L0_attn_D_skip, L0_attn_out_proj_w, L0_xattn_Wk, L0_xattn_Wv, L0_xattn_bv, L0_xattn_Wq, L0_xattn_bq, L0_xattn_Wo, L0_xattn_bo, L0_ffn_gate_w, L0_ffn_w1, L0_ffn_b1, L0_ffn_w2, L0_ffn_b2):
    import jax
    import jax.numpy as jnp

    def _L0_attn_ref(x, in_proj_w, conv_w, conv_b, x_proj_w, dt_proj_w, dt_proj_b, A_log, D_skip, out_proj_w):
        import jax, jax.numpy as jnp
        import numpy as np
        D_MODEL = 256
        N_LAYERS = 2
        D_STATE = 64
        D_CONV = 4
        EXPAND = 2
        D_INNER = EXPAND * D_MODEL
        DT_RANK = (D_MODEL + 15) // 16
        BATCH, SEQLEN = (2, 256)

        def _silu(x):
            return x * jax.nn.sigmoid(x)

        def _causal_dwconv(x, w, b):
            K = w.shape[-1]
            L = x.shape[1]
            xp = jnp.pad(x, ((0, 0), (K - 1, 0), (0, 0)))
            y = sum((xp[:, k:k + L, :] * w[:, k] for k in range(K)))
            return y + b

        def _selective_scan(u, dt, A, Bm, C, D_skip):
            B, L, dI = u.shape
            dS = A.shape[-1]

            def step(h, inp):
                u_t, dt_t, B_t, C_t = inp
                dA = jnp.exp(dt_t[:, :, None] * A)
                h = h * dA + (dt_t * u_t)[:, :, None] * B_t[:, None, :]
                y = jnp.einsum('bds,bs->bd', h, C_t)
                return (h, y)
            h0 = jnp.zeros((B, dI, dS), u.dtype)
            xs = (u.transpose(1, 0, 2), dt.transpose(1, 0, 2), Bm.transpose(1, 0, 2), C.transpose(1, 0, 2))
            _, ys = jax.lax.scan(step, h0, xs)
            return ys.transpose(1, 0, 2) + u * D_skip

        def _mamba_block(x, in_w, cw, cb, xp_w, dtw, dtb, A_log, D_skip, out_w):
            xz = jnp.einsum('bld,ed->ble', x, in_w)
            u, z = jnp.split(xz, 2, axis=-1)
            u = _silu(_causal_dwconv(u, cw, cb))
            x_dbl = jnp.einsum('bld,ed->ble', u, xp_w)
            dt, Bm, C = jnp.split(x_dbl, [DT_RANK, DT_RANK + D_STATE], axis=-1)
            dt = jax.nn.softplus(jnp.einsum('blr,dr->bld', dt, dtw) + dtb)
            A = -jnp.exp(A_log)
            y = _selective_scan(u, dt, A, Bm, C, D_skip)
            y = y * _silu(z)
            return jnp.einsum('bld,ed->ble', y, out_w)
        out = x
        for i in range(N_LAYERS):
            out = _mamba_block(out, in_proj_w[i], conv_w[i], conv_b[i], x_proj_w[i], dt_proj_w[i], dt_proj_b[i], A_log[i], D_skip[i], out_proj_w[i])
        return out

    def _L0_xattn_ref(k, v, q, Wk, Wv, bv, Wq, bq, Wo, bo):
        import jax, jax.numpy as jnp
        import numpy as np
        D_MODEL = 256
        B, S = (4, 512)
        kp = jnp.einsum('bsd,ed->bse', k, Wk)
        vp = jnp.einsum('bsd,ed->bse', v, Wv) + bv
        qp = jnp.einsum('bsd,ed->bse', q, Wq) + bq
        scale = 1.0 / jnp.sqrt(jnp.float32(kp.shape[-1]))
        scores = jnp.einsum('bqd,bkd->bqk', qp, kp) * scale
        probs = jax.nn.softmax(scores, axis=-1)
        ctx = jnp.einsum('bqk,bkd->bqd', probs, vp)
        return jnp.einsum('bqd,ed->bqe', ctx, Wo) + bo

    def _L0_ffn_ref(x, gate_w, w1, b1, w2, b2):
        import jax, jax.numpy as jnp
        import numpy as np
        D_MODEL = 256
        NUM_EXPERTS = 8
        HIDDEN = 1024
        TOP_K = 2
        B, S, D = x.shape
        xf = x.reshape(-1, D)
        T = xf.shape[0]
        gate_logits = xf @ gate_w.T
        gate_probs = jax.nn.softmax(gate_logits, axis=-1)
        topk_scores, topk_idx = jax.lax.top_k(gate_probs, TOP_K)
        topk_scores = topk_scores / jnp.sum(topk_scores, axis=-1, keepdims=True)
        combine = jnp.zeros((T, NUM_EXPERTS), dtype=x.dtype)
        combine = combine.at[jnp.arange(T)[:, None], topk_idx].set(topk_scores)
        h = jax.nn.relu(jnp.einsum('td,ehd->teh', xf, w1) + b1)
        expert_out = jnp.einsum('teh,edh->ted', h, w2) + b2
        out = jnp.einsum('ted,te->td', expert_out, combine)
        return out.reshape(B, S, D)
    x = _layernorm(x + _L0_attn_ref(x, L0_attn_in_proj_w, L0_attn_conv_w, L0_attn_conv_b, L0_attn_x_proj_w, L0_attn_dt_proj_w, L0_attn_dt_proj_b, L0_attn_A_log, L0_attn_D_skip, L0_attn_out_proj_w), axis=-1)
    x = _layernorm(x + _L0_xattn_ref(ctx_1024, ctx_1024, x, L0_xattn_Wk, L0_xattn_Wv, L0_xattn_bv, L0_xattn_Wq, L0_xattn_bq, L0_xattn_Wo, L0_xattn_bo), axis=-1)
    x = _layernorm(x + _L0_ffn_ref(x, L0_ffn_gate_w, L0_ffn_w1, L0_ffn_b1, L0_ffn_w2, L0_ffn_b2), axis=-1)
    return x

_drawn_inputs = setup_inputs


def setup_inputs(seed=0):
    import zlib

    import numpy as np

    out = dict(_drawn_inputs(seed))
    spreads = {'L0_attn_conv_b': (0.0, 0.1),
     'L0_attn_D_skip': (1.0, 0.2),
     'L0_xattn_bv': (0.0, 0.1),
     'L0_xattn_bq': (0.0, 0.1),
     'L0_xattn_bo': (0.0, 0.1)}
    factors = {}
    for name, (base, spread) in spreads.items():
        noise = np.random.default_rng([zlib.crc32(name.encode()), seed]).standard_normal(out[name].shape)
        drawn = base * np.exp(spread * noise) if base else spread * noise
        out[name] = jnp.asarray(drawn.astype(out[name].dtype))
    for name, factor in factors.items():
        out[name] = (out[name] * factor).astype(out[name].dtype)
    return out
```

```python
from contextlib import ExitStack

import numpy as np

import concourse.bass as bass
from concourse import mybir

F32 = mybir.dt.float32
BF16 = mybir.dt.bfloat16
ALU = mybir.AluOpType
ACT = mybir.ActivationFunctionType
AX_X = mybir.AxisListType.X

P = 128
ROWS, L, D = 8, 256, 256
LAYERS, DI, S, R, TAPS = 2, 512, 64, 16, 4
E, HID = 8, 1024
KD = D // P
KI = DI // P
KL = L // P
KH = HID // P
BANK = 512
HALF = S // 2
EPS = 1e-5
CG = 4
NA, NH, NHC = 3, 2, 2
NW = 3
DT0 = S
ONE = DT0 + R


class Token:

    def __init__(self, sem, value):
        self.sem, self.value = sem, value


class Buffer:

    def __init__(self, ap):
        self.ap, self.filled, self.read = ap, [], []

    def fill(self, *tokens):
        self.filled, self.read = list(tokens), []


class Queues:

    def __init__(self, nc, ctx):
        self.nc, self.ctx = nc, ctx
        self.queue = {e: [] for e in ("sync", "gpsimd", "scalar", "vector", "tensor")}
        self.sems, self.count, self.owner = {}, {}, {}

    def put(self, engine, stage, make, *waits, step=1):
        if stage is None:
            self.queue[engine].append((waits, make, None, 0))
            return None
        if stage not in self.sems:
            self.sems[stage] = self.ctx.enter_context(self.nc.semaphore(stage))
            self.count[stage], self.owner[stage] = 0, engine
        assert self.owner[stage] == engine
        self.count[stage] += step
        self.queue[engine].append((waits, make, self.sems[stage], step))
        return Token(self.sems[stage], self.count[stage])

    def run(self, engine, eng):
        seen = {}
        for waits, make, sem, step in self.queue[engine]:
            need = {}
            for w in waits:
                if w.value > max(seen.get(w.sem, 0), need.get(w.sem, 0)):
                    need[w.sem] = w.value
            for s, v in need.items():
                eng.wait_ge(s, v)
                seen[s] = v
            made = make(eng)
            if sem is not None:
                made.then_inc(sem, step)


def decoder_block(nc, io, out):
    ctx = ExitStack()
    with ctx:
        q = Queues(nc, ctx)
        put = q.put

        def sb(name, shape, dt=F32):
            return ctx.enter_context(nc.sbuf_tensor(name, shape, dt))

        def psum(name, shape):
            return ctx.enter_context(nc.psum_tensor(name, shape, F32))

        psY = psum("psY", [P, KL, DI])
        psU = psum("psU", [P, KI, L])
        psB = [psum(f"psB{i}", [P, BANK]) for i in range(2)]
        psG = [psum(f"psG{i}", [P, BANK]) for i in range(2)]
        dtuB = Buffer(psU)
        ysum = Buffer(psY)
        bbank = [Buffer(x) for x in psB]
        bank = [Buffer(x) for x in psG]

        w_in = sb("w_in", [P, LAYERS, KD, 2 * DI])
        w_x = sb("w_x", [P, LAYERS, KI, 6 * HALF + S + R])
        w_dt = sb("w_dt", [P, LAYERS, DI])
        w_out = sb("w_out", [P, LAYERS, KI, D])
        negA = sb("negA", [P, LAYERS, KI, S])
        conv_w = sb("conv_w", [P, LAYERS, KI, TAPS + 1])
        dskip = sb("dskip", [P, LAYERS, KI])
        diagD = sb("diagD", [P, LAYERS, KI, P])
        w_att = sb("w_att", [P, 4, KD, D])
        b_att = sb("b_att", [P, 2, KD])
        bo_row = sb("bo_row", [1, D])
        w_gate = sb("w_gate", [P, KD, E])
        b1 = sb("b1", [P, E, KH])
        b2 = sb("b2", [E, D])
        ident = sb("ident", [P, P])
        sel = sb("sel", [3 * HALF, HALF, P], BF16)
        ones_row = sb("ones_row", [1, P])
        neg_half = sb("neg_half", [P, KL])
        rank = sb("rank", [P, KL, E])

        xin = [Buffer(sb(f"xin{i}", [P, KD, L])) for i in range(4)]
        scratch = Buffer(sb("scratch", [P, KI, L]))
        u = [Buffer(sb(f"u{i}", [P, KI, L])) for i in range(2)]
        sz = [Buffer(sb(f"sz{i}", [P, KL, DI])) for i in range(2)]
        dt = [Buffer(sb(f"dt{i}", [P, KI, L])) for i in range(2)]
        dtu = [Buffer(sb(f"dtu{i}", [P, KI, L])) for i in range(2)]
        cdt = Buffer(sb("cdt", [P, L]))
        bparts = [Buffer(sb(f"bparts{i}", [3 * HALF, 2, L], BF16)) for i in range(2)]
        brest = Buffer(sb("brest", [3 * HALF, 2, L]))
        bmid = Buffer(sb("bmid", [3 * HALF, 2, L], BF16))
        dA = [Buffer(sb(f"dA{i}", [P, KI, L])) for i in range(NA)]
        h = [Buffer(sb(f"h{i}", [P, KI, L])) for i in range(NH)]
        hC = [Buffer(sb(f"hC{i}", [P, KI, L])) for i in range(NHC)]
        cb = [Buffer(sb(f"cb{i}", [P, CG, L])) for i in range(2)]
        gT = Buffer(sb("gT", [P, KL, DI]))
        g = scratch
        c_dram = [Buffer(nc.dram_tensor(f"c_dram{i}", [S, L], F32, kind="Internal").ap()) for i in range(2)]

        xrow = Buffer(sb("xrow", [P, KL, D]))
        ctxT = Buffer(sb("ctxT", [P, KD, L]))
        resid = Buffer(sb("resid", [P, KL, D]))
        x1 = Buffer(sb("x1", [P, KL, D]))
        x1T = Buffer(sb("x1T", [P, KD, L]))
        qT = Buffer(sb("qT", [P, KD, L]))
        kT = Buffer(sb("kT", [P, KD, L]))
        vv = Buffer(sb("vv", [P, KL, D]))
        prob = Buffer(sb("prob", [P, KL, L]))
        x2 = Buffer(sb("x2", [P, KL, D]))
        x2T = Buffer(sb("x2T", [P, KD, L]))
        hid = [Buffer(sb(f"hid{i}", [P, 2, L])) for i in range(2)]
        wexp = [Buffer(sb(f"wexp{i}", [P, 2 * HID])) for i in range(NW)]
        acc = Buffer(sb("acc", [P, KL, D]))
        fin = resid
        small = sb("small", [P, 64])
        stats = sb("stats", [P, KL, 6])
        gl = sb("gl", [P, 8, KL, E])
        combT = Buffer(sb("combT", [E, L]))

        loads = []

        def load(dst, name, queue="sync"):
            return put(queue, "weights_in" if queue == "sync" else "weights_in2",
                       lambda e: e.dma_start(dst, io[name]), step=16)

        def load_row(b):
            x = xin[b % 2]
            x.fill(put("sync", f"xT_in{b % 2}", lambda e: e.dma_start(x.ap[:, :, :], io["xT"][b]), *x.read, step=16))

        load_row(0)
        loads.append(load(w_in[:, :, :, :], "w_in"))
        w_in_ready = loads[-1]
        loads.append(load(conv_w[:, :, :, :], "conv"))
        loads.append(load(w_x[:, :, :, :], "w_x"))
        loads.append(load(w_dt[DT0:ONE + 1, :, :], "w_dt"))
        loads.append(load(negA[:, :, :, :], "A_log", "scalar"))
        a_in = loads[-1]
        loads.append(load(dskip[:, :, :], "D_skip", "scalar"))
        skip_in = loads[-1]
        loads.append(load(w_out[:, :, :, :], "w_out", "scalar"))
        loads.append(load(w_att[:, :, :, :], "w_att", "scalar"))
        loads.append(load(b_att[:, :, :], "b_att", "scalar"))
        loads.append(load(bo_row[:, :], "bo", "scalar"))
        loads.append(load(w_gate[:, :, :], "w_gate", "scalar"))
        loads.append(load(b1[:, :, :], "b1", "scalar"))
        loads.append(load(b2[:, :], "b2", "scalar"))
        w_ready = [[t for t in loads if t.sem is s][-1] for s in (w_in_ready.sem, a_in.sem)]
        w_in_ready = w_ready[0]

        done = []

        def pool(make, *waits):
            done.append(put("gpsimd", "setup", make, *waits, *done[-1:]))

        pool(lambda e: e.memset(ident[:, :], 0.0))
        pool(lambda e: e.affine_select(
            out=ident[:, :], in_=ident[:, :], compare_op=ALU.not_equal, fill=1.0, base=0,
            pattern=[[-1, P]], channel_multiplier=1))
        pool(lambda e: e.memset(sel[:, :, :], 0.0))
        for part in range(3):
            pool(lambda e, part=part: e.affine_select(
                out=sel[:, :, :], in_=sel[:, :, :], compare_op=ALU.not_equal, fill=1.0,
                base=-HALF * part, pattern=[[-1, HALF], [0, P]], channel_multiplier=1))
        pool(lambda e: e.memset(ones_row[:, :], 1.0))
        pool(lambda e: e.memset(neg_half[:, :], -0.5))
        pool(lambda e: e.memset(cdt.ap[DT0:DT0 + 32, :], 1.0))
        for i in range(E):
            pool(lambda e, i=i: e.memset(rank[:, :, i:i + 1], float(E - i)))
        for a in dA:
            pool(lambda e, a=a: e.memset(a.ap[:, :, 0:1], 0.0))
        for l in range(LAYERS):
            for c in range(KI):
                pool(lambda e, l=l, c=c: e.tensor_scalar(
                    diagD[:, l, c, :], ident[:, :], dskip[:, l, c:c + 1], None, ALU.mult), w_ready[1])
        setup = done[-1]
        cdt.fill(setup)
        put("scalar", None, lambda e: e.preload_act_table_set("natural_log_exp_and_others"))
        expA = put("scalar", "expA", lambda e: e.activation(
            negA[:, :, :, :], negA[:, :, :, :], ACT.Exp), w_ready[1])
        A_ready = put("vector", "negA", lambda e: e.tensor_scalar(
            negA[:, :, :, :], negA[:, :, :, :], -1.0, None, ALU.mult), expA)


        def mm(stage, dst, pairs, *waits, start=True, check=False):
            n = len(pairs)
            for i, (lhs, rhs) in enumerate(pairs):
                t = put("tensor", stage if i == n - 1 else None,
                        lambda e, lhs=lhs, rhs=rhs, i=i: e.matmul(
                            dst, lhs, rhs, start=start and i == 0, stop=i == n - 1,
                            skip_group_check=check), *(waits if i == 0 else ()))
            return t

        def transpose(stage, dst, src, *waits):
            return put("tensor", stage, lambda e: e.transpose(dst, src, ident[:, :]), *waits)

        def act(stage, dst, src, func, *waits, **kw):
            return put("scalar", stage, lambda e: e.activation(dst, src, func, **kw), *waits)

        def pre(l, b, n, x):
            su, ssz, sdt, sdtu, sbp = u[n % 2], sz[n % 2], dt[n % 2], dtu[n % 2], bparts[n % 2]
            toks = []
            for tc in range(KL):
                k = bank[tc]
                t = mm("in_proj", k.ap[:, :], [(x.ap[:, d, tc * P:(tc + 1) * P], w_in[:, l, d, DI:2 * DI])
                                               for d in range(KD)], *x.filled, *k.read, *w_ready)
                yield 1700
                s = act("silu", ssz.ap[:, tc, :], k.ap[:, :], ACT.Silu, t, *ssz.read)
                toks.append(s)
                k.fill(t)
                k.read = [s]
            ssz.fill(*toks)
            conv = []
            for half in range(2):
                k = bank[half]
                for i in range(2):
                    c = 2 * half + i
                    t = mm("in_proj", k.ap[:, i * L:(i + 1) * L],
                           [(w_in[:, l, d, c * P:(c + 1) * P], x.ap[:, d, :]) for d in range(KD)], *k.read)
                x.read = [t]
                yield 1700
                for i in range(2):
                    c = 2 * half + i
                    src, dst = k.ap[:, i * L:(i + 1) * L], scratch.ap[:, c, :]
                    v = put("vector", "conv", lambda e, src=src, dst=dst, c=c: e.tensor_scalar(
                        dst, src, conv_w[:, l, c, TAPS - 1:TAPS], conv_w[:, l, c, TAPS:TAPS + 1], ALU.mult, ALU.add),
                        t, *scratch.read)
                    for j in range(1, TAPS):
                        v = put("vector", "conv", lambda e, src=src, dst=dst, c=c, j=j: e.scalar_tensor_tensor(
                            out=dst[:, j:], in0=src[:, :L - j], scalar=conv_w[:, l, c, TAPS - 1 - j:TAPS - j],
                            in1=dst[:, j:], op0=ALU.mult, op1=ALU.add), v)
                k.read = [v]
            s = act("silu", su.ap[:, :, :], scratch.ap[:, :, :], ACT.Silu, v, *su.read)
            su.fill(s)
            scratch.fill(v)
            scratch.read = [s]
            put("scalar", None, lambda e: e.preload_act_table_set("natural_log_exp_and_others"))
            yield 0
            kb, kc = bank
            for half in range(2):
                t = mm("x_proj", kb.ap[0:3 * HALF, half * L:(half + 1) * L],
                       [(w_x[:, l, c, half * 3 * HALF:(half + 1) * 3 * HALF], su.ap[:, c, :]) for c in range(KI)],
                       s, *kb.read)
                yield 1700
            tc_ = mm("x_proj", kc.ap[0:S + R, 0:L], [(w_x[:, l, c, 6 * HALF:6 * HALF + S + R], su.ap[:, c, :])
                                                     for c in range(KI)], *kc.read)
            su.read = [tc_]
            yield 1700
            b3 = kb.ap[0:3 * HALF, :].rearrange("p (a t) -> p a t", a=2)
            hi = act("b_hi", sbp.ap[:, :, :], b3, ACT.Copy, t, *sbp.read)
            cs = act("c_dt", cdt.ap[0:S + R, :], kc.ap[0:S + R, 0:L], ACT.Copy, tc_, *cdt.read, *cdt.filled)
            kc.read = [cs]
            cdt.fill(cs)
            r1 = put("vector", "b_rest", lambda e: e.tensor_tensor(brest.ap[:, :, :], b3, sbp.ap[:, :, :],
                                                                   ALU.subtract), hi, *brest.read)
            kb.read = [r1]
            cd = c_dram[n % 2]
            cd.fill(put("sync", "c_out", lambda e: e.dma_start(cd.ap, cdt.ap[0:S, :]), cs, *cd.read, step=16))
            yield 0
            mid = act("b_mid", bmid.ap[:, :, :], brest.ap[:, :, :], ACT.Copy, r1, *bmid.read)
            r2 = put("vector", "b_rest", lambda e: e.tensor_tensor(brest.ap[:, :, :], brest.ap[:, :, :],
                                                                   bmid.ap[:, :, :], ALU.subtract), mid, r1)
            dts = []
            for half in range(2):
                k = bank[half]
                for i in range(2):
                    c = 2 * half + i
                    t = mm("dt_proj", k.ap[:, i * L:(i + 1) * L],
                           [(w_dt[DT0:ONE + 1, l, c * P:(c + 1) * P], cdt.ap[DT0:ONE + 1, :])], cs, *k.read)
                dts.append(t)
            cdt.read = [cd.filled[0], t]
            yield 1700
            m1 = act("b_lo", sbp.ap[HALF:2 * HALF, :, :], bmid.ap[HALF:2 * HALF, :, :], ACT.Copy, r2, hi)
            m2 = act("b_lo", sbp.ap[2 * HALF:3 * HALF, :, :], brest.ap[2 * HALF:3 * HALF, :, :], ACT.Copy, r2, r1)
            bmid.read, brest.read = [m1], [m2]
            sbp.fill(m2)
            ab = [act("softplus", scratch.ap[:, 2 * i:2 * i + 2, :],
                      bank[i].ap[:, :].rearrange("p (a t) -> p a t", a=2), ACT.Abs, dts[i], *scratch.read)
                  for i in range(2)]
            ex = act("softplus", scratch.ap[:, :, :], scratch.ap[:, :, :], ACT.Exp, *ab, scale=-1.0)
            ln = act("softplus", scratch.ap[:, :, :], scratch.ap[:, :, :], ACT.Ln, ex, bias=1.0)
            yield 0
            for i in range(2):
                src = bank[i].ap[:, :].rearrange("p (a t) -> p a t", a=2)
                v = put("vector", "dt", lambda e, i=i, src=src: e.scalar_tensor_tensor(
                    out=sdt.ap[:, 2 * i:2 * i + 2, :], in0=src, scalar=0.0, in1=scratch.ap[:, 2 * i:2 * i + 2, :],
                    op0=ALU.max, op1=ALU.add), ln, *sdt.read)
                bank[i].read = [v]
            scratch.fill(ln)
            scratch.read = [v]
            sdt.fill(v)
            w = put("vector", "dtu", lambda e: e.tensor_tensor(sdtu.ap[:, :, :], sdt.ap[:, :, :], su.ap[:, :, :],
                                                               ALU.mult), v, s, *sdtu.read)
            sdtu.fill(w)
            su.read.append(w)
            yield 0

        def gate_and_turn(l, n):
            su, ssz = u[n % 2], sz[n % 2]
            toks = []
            for tc in range(KL):
                for c in range(KI):
                    t = put("tensor", "y_done", lambda e, tc=tc, c=c: e.matmul(
                        psY[:, tc, c * P:(c + 1) * P], su.ap[:, c, tc * P:(tc + 1) * P], diagD[:, l, c, :],
                        start=False, stop=True, skip_group_check=True), *su.filled, setup)
                toks.append(put("vector", "gate", lambda e, tc=tc: e.tensor_tensor(
                    gT.ap[:, tc, :], psY[:, tc, :], ssz.ap[:, tc, :], ALU.mult), t, *ssz.filled, *gT.read))
            su.read.append(t)
            ysum.read = [toks[-1]]
            gT.fill(*toks)
            ssz.read = [toks[-1]]

        def turned():
            outs = []
            for half in range(2):
                k = bank[half]
                for i in range(2):
                    for tc in range(KL):
                        c = 2 * half + i
                        t = transpose("g_turn", k.ap[:, i * L + tc * P:i * L + (tc + 1) * P],
                                      gT.ap[:, tc, c * P:(c + 1) * P], *gT.filled, *k.read, setup)
                s = act("g", g.ap[:, 2 * half:2 * half + 2, :], k.ap[:, :].rearrange("p (a t) -> p a t", a=2),
                        ACT.Copy, t, *g.read)
                k.read = [s]
                outs.append(s)
            gT.read = [t]
            g.fill(*outs)

        def post_inner(l, n, nxt):
            turned()
            yield 900
            k = bank[0]
            for i in range(KD):
                t = mm("out_proj", k.ap[:, i * L:(i + 1) * L],
                       [(w_out[:, l, c, i * P:(i + 1) * P], g.ap[:, c, :]) for c in range(KI)], *g.filled, *k.read)
                yield 1700
            g.read = [t]
            s = act("x_next", nxt.ap[:, :, :], k.ap[:, :].rearrange("p (a t) -> p a t", a=2), ACT.Copy, t, *nxt.read)
            k.read = [s]
            nxt.fill(s)

        def layernorm(src, dst, where, *waits):
            mv = small[:, where:where + 4].rearrange("p (c s) -> p c s", c=KL)
            rs = small[:, where + 4:where + 6]
            toks = []
            for tc in range(KL):
                v = put("vector", "norm", lambda e, tc=tc: e.bn_stats(stats[:, tc, :], src.ap[:, tc, :]),
                        *waits, *src.filled)
                toks.append(put("vector", "norm", lambda e, tc=tc: e.bn_aggr(mv[:, tc, :], stats[:, tc, :]), v))
            v = put("vector", "norm", lambda e: e.tensor_scalar(mv[:, :, 1], mv[:, :, 1], EPS, None, ALU.add), *toks)
            p = put("gpsimd", "rstd", lambda e: e.tensor_tensor(rs, mv[:, :, 1], neg_half[:, :], ALU.pow), v, setup)
            for tc in range(KL):
                v = put("vector", "norm", lambda e, tc=tc: e.tensor_scalar(
                    dst.ap[:, tc, :], src.ap[:, tc, :], mv[:, tc, 0:1], rs[:, tc:tc + 1], ALU.subtract, ALU.mult),
                    p, *dst.read)
            dst.fill(v)
            src.read = [v]

        def load_ctx(b):
            ctxT.fill(put("sync", "ctx_in", lambda e: e.dma_start(ctxT.ap[:, :, :], io["ctxT"][b]), *ctxT.read, step=16))
            xrow.fill(put("sync", "xrow_in", lambda e: e.dma_start(xrow.ap[:, :, :], io["x"][b]), *xrow.read, step=16))

        def post_outer(l, n):
            turned()
            yield 900
            k = bank[0]
            for tc in range(KL):
                t = mm("out_proj", k.ap[:, tc * D:(tc + 1) * D],
                       [(g.ap[:, c, tc * P:(tc + 1) * P], w_out[:, l, c, :]) for c in range(KI)], *g.filled, *k.read)
                yield 1700
            g.read = [t]
            v = put("vector", "resid", lambda e: e.tensor_tensor(
                resid.ap[:, :, :], k.ap[:, :].rearrange("p (a t) -> p a t", a=2), xrow.ap[:, :, :], ALU.add),
                t, *xrow.filled, *resid.read)
            k.read = [v]
            xrow.read = [v]
            resid.fill(v)
            layernorm(resid, x1, 0)
            yield 0

        def turn_rows(stage, src, dst, k):
            for d in range(KD):
                for tc in range(KL):
                    t = transpose(stage, k.ap[:, d * L + tc * P:d * L + (tc + 1) * P],
                                  src.ap[:, tc, d * P:(d + 1) * P], *src.filled, *k.read, setup)
            src.read.append(t)
            s = act("turned", dst.ap[:, :, :], k.ap[:, :].rearrange("p (a t) -> p a t", a=2), ACT.Copy, t, *dst.read)
            k.read = [s]
            dst.fill(s)

        def attention(b):
            WQ, WK, WV, WO = range(4)
            two = lambda k: k.ap[:, :].rearrange("p (a t) -> p a t", a=2)
            k = bank[1]
            for i in range(KD):
                t = mm("attn", k.ap[:, i * L:(i + 1) * L],
                       [(w_att[:, WK, d, i * P:(i + 1) * P], ctxT.ap[:, d, :]) for d in range(KD)],
                       *ctxT.filled, *k.read, *w_ready)
            s = act("kv", kT.ap[:, :, :], two(k), ACT.Copy, t, *kT.read)
            k.read = [s]
            kT.fill(s)
            yield 1700
            k = bank[0]
            for tc in range(KL):
                t = mm("attn", k.ap[:, tc * D:(tc + 1) * D],
                       [(ctxT.ap[:, d, tc * P:(tc + 1) * P], w_att[:, WV, d, :]) for d in range(KD)], *k.read)
            ctxT.read = [t]
            s = act("kv", vv.ap[:, :, :], two(k), ACT.Copy, t, *vv.read)
            k.read = [s]
            vv.fill(s)
            yield 1700
            turn_rows("attn", x1, x1T, bank[1])
            yield 500
            k = bank[0]
            for i in range(KD):
                t = mm("attn", k.ap[:, i * L:(i + 1) * L],
                       [(w_att[:, WQ, d, i * P:(i + 1) * P], x1T.ap[:, d, :]) for d in range(KD)],
                       *x1T.filled, *k.read)
            x1T.read = [t]
            for i in range(KD):
                s = act("q", qT.ap[:, i, :], k.ap[:, i * L:(i + 1) * L], ACT.Identity, t, *qT.read,
                        bias=b_att[:, 0, i:i + 1])
            k.read = [s]
            qT.fill(s)
            yield 1700
            scale = float(D) ** -0.5
            k = bank[1]
            for tc in range(KL):
                t = mm("attn", k.ap[:, tc * L:(tc + 1) * L],
                       [(qT.ap[:, d, tc * P:(tc + 1) * P], kT.ap[:, d, :]) for d in range(KD)],
                       *qT.filled, *kT.filled, *k.read)
            qT.read, kT.read = [t], [t]
            mx, nm, rsum, rinv = (small[:, 8 + 2 * i:10 + 2 * i] for i in range(4))
            v = put("vector", "softmax", lambda e: e.tensor_reduce(mx, two(bank[1]), AX_X, ALU.max), t)
            v = put("vector", "softmax", lambda e: e.tensor_scalar(nm, mx, -scale, None, ALU.mult), v)
            yield 1700
            for tc in range(KL):
                s = act("prob", prob.ap[:, tc, :], k.ap[:, tc * L:(tc + 1) * L], ACT.Exp, v, *prob.read,
                        scale=scale, bias=nm[:, tc:tc + 1], accum_out=rsum[:, tc:tc + 1])
            k.read = [s]
            v = put("vector", "softmax", lambda e: e.reciprocal(rinv, rsum), s)
            for tc in range(KL):
                w = put("vector", "softmax", lambda e, tc=tc: e.tensor_scalar(
                    prob.ap[:, tc, :], prob.ap[:, tc, :], rinv[:, tc:tc + 1], None, ALU.mult), v)
            prob.fill(w)
            yield 0
            k = bank[0]
            for kc in range(KL):
                for tc in range(KL):
                    t = transpose("attn", k.ap[:, kc * L + tc * P:kc * L + (tc + 1) * P],
                                  prob.ap[:, tc, kc * P:(kc + 1) * P], *prob.filled, *k.read)
            prob.read = [t]
            s = act("turned", x1T.ap[:, :, :], two(k), ACT.Copy, t, *x1T.read)
            k.read = [s]
            x1T.fill(s)
            yield 500
            k = bank[1]
            for i in range(KD):
                t = mm("attn", k.ap[:, i * L:(i + 1) * L],
                       [(vv.ap[:, kc, i * P:(i + 1) * P], x1T.ap[:, kc, :]) for kc in range(KL)],
                       *x1T.filled, *vv.filled, *k.read)
            vv.read = [t]
            x1T.read = [t]
            for i in range(KD):
                s = act("q", qT.ap[:, i, :], k.ap[:, i * L:(i + 1) * L], ACT.Identity, t, *qT.read,
                        bias=b_att[:, 1, i:i + 1])
            k.read = [s]
            qT.fill(s)
            yield 1700
            k = bank[0]
            for tc in range(KL):
                t = mm("attn", k.ap[:, tc * D:(tc + 1) * D],
                       [(qT.ap[:, d, tc * P:(tc + 1) * P], w_att[:, WO, d, :]) for d in range(KD)]
                       + [(ones_row[:, :], bo_row[:, :])], *qT.filled, *k.read)
            qT.read = [t]
            v = put("vector", "resid", lambda e: e.tensor_tensor(
                resid.ap[:, :, :], two(bank[0]), x1.ap[:, :, :], ALU.add), t, *x1.filled, *resid.read)
            k.read = [v]
            x1.read.append(v)
            resid.fill(v)
            yield 2500
            layernorm(resid, x2, 16)
            yield 0

        def route(b):
            turn_rows("moe_turn", x2, x2T, bank[1])
            yield 500
            k = bank[0]
            for tc in range(KL):
                t = mm("gate_mm", k.ap[:, tc * E:(tc + 1) * E],
                       [(x2T.ap[:, d, tc * P:(tc + 1) * P], w_gate[:, d, :]) for d in range(KD)],
                       *x2T.filled, *k.read)
            x2T.read = [t]
            lg = k.ap[:, 0:KL * E].rearrange("p (c e) -> p c e", c=KL)
            pr, w0, key, hot1, hot2, hot = (gl[:, i, :, :] for i in range(6))
            m = lambda i: small[:, 24 + 2 * i:26 + 2 * i]
            wide = lambda x: x.rearrange("p (c e) -> p c e", e=1).to_broadcast([P, KL, E])

            def v(make, *waits):
                v.last = put("vector", "route", make, *waits, *([v.last] if v.last else []))
                return v.last

            v.last = None
            v(lambda e: e.tensor_reduce(m(0), lg, AX_X, ALU.max), t, *combT.read)
            a = v(lambda e: e.tensor_tensor(w0, lg, wide(m(0)), ALU.subtract))
            k.read = [a]
            s = act("route_exp", pr, w0, ACT.Exp, a)
            v(lambda e: e.tensor_reduce(m(1), pr, AX_X, ALU.add), s)
            v(lambda e: e.reciprocal(m(2), m(1)))
            v(lambda e: e.tensor_tensor(pr, pr, wide(m(2)), ALU.mult))
            yield 200
            src = pr
            for hotn, mi in ((hot1, 3), (hot2, 4)):
                v(lambda e, src=src, mi=mi: e.tensor_reduce(m(mi), src, AX_X, ALU.max))
                v(lambda e, src=src, mi=mi: e.tensor_tensor(key, src, wide(m(mi)), ALU.is_equal))
                v(lambda e: e.tensor_tensor(key, key, rank[:, :, :], ALU.mult))
                v(lambda e: e.tensor_reduce(m(5), key, AX_X, ALU.max))
                v(lambda e, hotn=hotn: e.tensor_tensor(hotn, key, wide(m(5)), ALU.is_equal))
                if src is pr:
                    v(lambda e: e.scalar_tensor_tensor(out=w0, in0=hot1, scalar=-2.0, in1=pr,
                                                       op0=ALU.mult, op1=ALU.add))
                    src = w0
                yield 0
            v(lambda e: e.tensor_tensor(hot, hot1, hot2, ALU.add))
            v(lambda e: e.tensor_tensor(hot, hot, pr, ALU.mult))
            v(lambda e: e.tensor_tensor(m(6), m(3), m(4), ALU.add))
            v(lambda e: e.reciprocal(m(7), m(6)))
            a = v(lambda e: e.tensor_tensor(hot, hot, wide(m(7)), ALU.mult), *acc.read)
            yield 0
            k = bank[1]
            for tc in range(KL):
                t = put("tensor", "moe_turn", lambda e, tc=tc, k=k: e.transpose(
                    k.ap[0:E, tc * P:(tc + 1) * P], hot[:, tc, :], ident[:, :]), a, *k.read)
            s = act("combT", combT.ap[:, :], k.ap[0:E, 0:L], ACT.Copy, t, *combT.read)
            combT.fill(s)
            k.read = [s]
            yield 200
            k = bank[0]
            for tc in range(KL):
                t = mm("gate_mm", k.ap[:, tc * D:(tc + 1) * D],
                       [(combT.ap[:, tc * P:(tc + 1) * P], b2[:, :])], s, *k.read)
            combT.read = [t]
            w = put("vector", "acc", lambda e: e.tensor_tensor(
                acc.ap[:, :, :], bank[0].ap[:, :].rearrange("p (a t) -> p a t", a=2), x2.ap[:, :, :], ALU.add),
                t, *x2.filled, *acc.read)
            k.read = [w]
            x2.read.append(w)
            acc.fill(w)
            yield 900

        def load_half(b, e, half):
            n = (b * E + e) * 2 + half
            w = wexp[n % NW]
            w.fill(put("sync", f"wexp_in{n % NW}", lambda en: en.dma_start(w.ap[:, :], io["w_exp"][e, half]),
                       *w.read, step=16))

        halves = [(b, e, f) for b in range(ROWS) for e in range(E) for f in range(2)]

        def experts(b, which):
            hot = gl[:, 5, :, :]
            HB, OB = bank[0], bank[1]
            for e in which:
                pending = []
                first = True

                def out_pair():
                    nonlocal first
                    w, j, hb, last = pending.pop(0)
                    for i in range(2):
                        for tc in range(KL):
                            t = put("tensor", "moe_out", lambda en, i=i, tc=tc, st=first: en.matmul(
                                OB.ap[:, tc * D:(tc + 1) * D], hb.ap[:, i, tc * P:(tc + 1) * P],
                                w.ap[:, HID + (j + i) * D:HID + (j + i + 1) * D], start=st, stop=last,
                                skip_group_check=True), *hb.filled, *(OB.read if first else ()))
                            first = False
                    hb.read = [t]
                    w.read = [t]
                    return t

                for pair in range(KH // 2):
                    half, j = pair // 2, 2 * (pair % 2)
                    n = (b * E + e) * 2 + half
                    w = wexp[n % NW]
                    w1 = w.ap[:, 0:HID].rearrange("p (k m) -> p k m", k=KD)
                    hb = hid[pair % 2]
                    for i in range(2):
                        t = mm("moe_hid", HB.ap[:, i * L:(i + 1) * L],
                               [(w1[:, d, (j + i) * P:(j + i + 1) * P], x2T.ap[:, d, :]) for d in range(KD)],
                               *w.filled, *HB.read)
                    for i in range(2):
                        c = 2 * pair + i
                        s = act("moe_relu", hb.ap[:, i, :], HB.ap[:, i * L:(i + 1) * L], ACT.Relu, t, *hb.read,
                                bias=b1[:, e, c:c + 1])
                    hb.fill(s)
                    HB.read = [s]
                    if pair == 0:
                        yield 1700
                    pending.append((w, j, hb, pair == KH // 2 - 1))
                    if pair > 0:
                        t2 = out_pair()
                        if pair % 2 == 0:
                            at = (b * E + e) * 2 + half - 1 + NW
                            if at < len(halves):
                                load_half(*halves[at])
                        yield 3400
                x2T.read.append(t)
                t = out_pair()
                at = (b * E + e) * 2 + 1 + NW
                if at < len(halves):
                    load_half(*halves[at])
                for tc in range(KL):
                    v = put("vector", "acc", lambda en, tc=tc, e=e: en.scalar_tensor_tensor(
                        out=acc.ap[:, tc, :], in0=OB.ap[:, tc * D:(tc + 1) * D], scalar=hot[:, tc, e:e + 1],
                        in1=acc.ap[:, tc, :], op0=ALU.mult, op1=ALU.add), t, *acc.filled)
                OB.read = [v]
                acc.fill(v)
                yield 1700

        def finish(b):
            layernorm(acc, fin, 40)
            o = put("sync", "out", lambda e: e.dma_start(out[b], fin.ap[:, :, :]), *fin.filled, step=16)
            fin.read = [o]
            finish.last = o
            yield 0


        def scan_steps(l, n):
            sdt, sdtu, sbp, cd = dt[n % 2], dtu[n % 2], bparts[n % 2], c_dram[n % 2]
            y_read = list(ysum.read)

            def spread_b(pair):
                k = bbank[pair % 2]
                for i in range(2):
                    s = 2 * pair + i
                    t = put("tensor", "b_wide", lambda e, s=s, i=i: e.matmul(
                        k.ap[:, i * L:(i + 1) * L], sel[:, s % HALF, :], sbp.ap[:, s // HALF, :],
                        start=True, stop=True), *sbp.filled, *k.read, setup)
                k.fill(t)
                sbp.read = [t]

            def load_c(group):
                k = cb[group % 2]
                src = cd.ap[group * CG:(group + 1) * CG, :].rearrange("(a s) t -> a s t", a=1)
                k.fill(put("sync", f"c_in{group % 2}", lambda e: e.dma_start(
                    k.ap[:, :, :], src.to_broadcast([P, CG, L])), *cd.filled, *k.read, step=16))
                cd.read = [k.filled[0]]

            load_c(0)
            load_c(1)
            spread_b(0)
            spread_b(1)
            for s in range(S):
                a, hh, hc = dA[s % NA], h[s % NH], hC[s % NHC]
                kb, kc = bbank[(s // 2) % 2], cb[(s // CG) % 2]
                for c in range(KI):
                    t = act("dA", a.ap[:, c, 1:L], sdt.ap[:, c, 1:L], ACT.Exp, *sdt.filled, *a.read, A_ready, setup,
                            scale=negA[:, l, c, s:s + 1])
                a.fill(t)
                wide = kb.ap[:, (s % 2) * L:(s % 2 + 1) * L].rearrange("p (a t) -> p a t", a=1)
                m = put("vector", "dtuB", lambda e, wide=wide: e.tensor_tensor(
                    psU[:, :, :], sdtu.ap[:, :, :], wide.to_broadcast([P, KI, L]), ALU.mult),
                    *kb.filled, *sdtu.filled, *dtuB.read)
                kb.read = [m]
                r = put("vector", "scan", lambda e, a=a, hh=hh: e.tensor_tensor_scan(
                    hh.ap.rearrange("p c t -> p (c t)"), a.ap.rearrange("p c t -> p (c t)"),
                    psU.rearrange("p c t -> p (c t)"), 0.0, ALU.mult, ALU.add), t, m, *hh.read)
                dtuB.read, a.read = [r], [r]
                hh.fill(r)
                cw = kc.ap[:, s % CG:s % CG + 1, :]
                p = put("gpsimd", "hC", lambda e, hc=hc, hh=hh, cw=cw: e.tensor_tensor(
                    hc.ap[:, :, :], hh.ap[:, :, :], cw.to_broadcast([P, KI, L]), ALU.mult), r, *kc.filled, *hc.read)
                hh.read = [p]
                kc.read = [p]
                hc.fill(p)
                if s % CG == CG - 1 and s // CG + 2 < S // CG:
                    load_c(s // CG + 2)
                for tc in range(KL):
                    for c in range(KI):
                        x = put("tensor", "y_sum" if (tc, c) == (KL - 1, KI - 1) else None,
                                lambda e, s=s, tc=tc, c=c, hc=hc: e.matmul(
                                    psY[:, tc, c * P:(c + 1) * P], hc.ap[:, c, tc * P:(tc + 1) * P], ident[:, :],
                                    start=s == 0 and c == 0, stop=False, is_transpose=True,
                                    skip_group_check=True), *hc.filled, *(y_read if s == 0 else ()), setup)
                hc.read = [x]
                if s % 2 == 1 and s // 2 + 2 < S // 2:
                    spread_b(s // 2 + 2)
                yield
            sdt.read, sdtu.read = [t], [m]

        jobs = [(0, 0)]
        for b in range(1, ROWS):
            jobs += [(0, b), (1, b - 1)]
        jobs.append((1, ROWS - 1))

        nxt = lambda b: xin[2 + b % 2]

        def source(l, b):
            return xin[b % 2] if l == 0 else nxt(b)

        for i in range(NW):
            load_half(*halves[i])
        for _ in pre(0, 0, 0, xin[0]):
            pass
        backlog = []

        for n, (l, b) in enumerate(jobs):
            urgent = []
            if n > 0:
                pl, pb = jobs[n - 1]
                if pl == 0:
                    urgent.append(post_inner(pl, n - 1, nxt(pb)))
                else:
                    urgent.append(post_outer(pl, n - 1))
            if n + 1 < len(jobs):
                nl, nb = jobs[n + 1]
                if nl == 0:
                    load_row(nb)
                urgent.append(pre(nl, nb, n + 1, source(nl, nb)))
            def work(urgent=urgent):
                for gen in urgent:
                    yield from gen

            todo = [work()]
            if n > 0 and jobs[n - 1][0] == 1:
                pb = jobs[n - 1][1]
                backlog += [attention(pb), route(pb)] + [experts(pb, [e]) for e in range(E)] + [finish(pb)]
            budget = 2 if l == 0 else 99
            todo += backlog[:]
            quota = 5 if n > 0 and jobs[n - 1][0] == 1 and n + 1 < len(jobs) and l == 0 else len(backlog)
            todo, backlog = [todo[0]] + backlog[:quota], backlog[quota:]

            def units(todo=todo):
                for gen in todo:
                    yield from gen

            est = 8 * 1700 + 8 * 1700 + sum(13600 + 1000 for _ in todo[1:])
            per_step = est / (S - 2)
            gen, owed, more = units(), 0.0, True
            for _ in scan_steps(l, n):
                owed += per_step
                while more and owed > 0:
                    got = next(gen, None)
                    if got is None:
                        more = False
                    else:
                        owed -= max(got, 300)
            for _ in gen:
                pass
            if l == 1:
                load_ctx(b)
            gate_and_turn(l, n)
        for gen in [post_outer(1, len(jobs) - 1), *backlog, attention(ROWS - 1), route(ROWS - 1),
                    experts(ROWS - 1, range(E)), finish(ROWS - 1)]:
            for _ in gen:
                pass
        q.queue["sync"].append(((Token(q.sems["out"], q.count["out"]), Token(q.sems["c_out"], q.count["c_out"])),
                                lambda e: None, None, 0))

        block = ctx.enter_context(nc.Block())

        @block.sync
        def _(eng):
            q.run("sync", eng)

        @block.gpsimd
        def _(eng):
            q.run("gpsimd", eng)

        @block.scalar
        def _(eng):
            q.run("scalar", eng)

        @block.vector
        def _(eng):
            q.run("vector", eng)

        @block.tensor
        def _(eng):
            q.run("tensor", eng)




def lay_out(i):
    c = np.ascontiguousarray

    def chunks(w):
        *lead, k, n = w.shape
        w = w.reshape(*lead, k // P, P, n)
        return c(np.moveaxis(w, -2, 0))

    x, ctx = i["x"], i["ctx_1024"]
    rowsT = lambda a: c(a.transpose(0, 2, 1).reshape(ROWS, KD, P, L).transpose(0, 2, 1, 3))
    rows = lambda a: c(a.reshape(ROWS, KL, P, D).transpose(0, 2, 1, 3))
    xp = i["L0_attn_x_proj_w"]
    Bw, Cw, dtw = xp[:, R:R + S], xp[:, R + S:], xp[:, :R]
    lo, hi = Bw[:, :HALF], Bw[:, HALF:]
    wx = np.concatenate([lo, lo, lo, hi, hi, hi, Cw, dtw], axis=1)
    w_dt = np.concatenate([i["L0_attn_dt_proj_w"].transpose(0, 2, 1), i["L0_attn_dt_proj_b"][:, None, :]], axis=1)
    conv = np.concatenate([i["L0_attn_conv_w"], i["L0_attn_conv_b"][:, :, None]], axis=2)
    w1 = i["L0_ffn_w1"].transpose(0, 2, 1).reshape(E, KD, P, 2, HID // 2).transpose(0, 3, 2, 1, 4)
    w2 = i["L0_ffn_w2"].transpose(0, 2, 1).reshape(E, 2, KH // 2, P, D).transpose(0, 1, 3, 2, 4)
    w_exp = np.concatenate([w1.reshape(E, 2, P, HID), w2.reshape(E, 2, P, HID)], axis=3)
    att = np.stack([i[f"L0_xattn_W{k}"].T for k in "qkvo"])
    return {
        "xT": rowsT(x), "x": rows(x), "ctxT": rowsT(ctx),
        "w_in": chunks(i["L0_attn_in_proj_w"].transpose(0, 2, 1)),
        "conv": chunks(conv),
        "w_x": chunks(wx.transpose(0, 2, 1)),
        "w_dt": c(w_dt.transpose(1, 0, 2)),
        "A_log": chunks(i["L0_attn_A_log"]),
        "D_skip": c(i["L0_attn_D_skip"].reshape(LAYERS, KI, P).transpose(2, 0, 1)),
        "w_out": chunks(i["L0_attn_out_proj_w"].transpose(0, 2, 1)),
        "w_att": chunks(att),
        "b_att": c(np.stack([i["L0_xattn_bq"], i["L0_xattn_bv"]]).reshape(2, KD, P).transpose(2, 0, 1)),
        "bo": c(i["L0_xattn_bo"].reshape(1, D)),
        "w_gate": chunks(i["L0_ffn_gate_w"].T),
        "b1": c(i["L0_ffn_b1"].reshape(E, KH, P).transpose(2, 0, 1)),
        "b2": c(i["L0_ffn_b2"]),
        "w_exp": c(w_exp),
    }


def kernel(**inputs):
    import concourse.bacc as bacc
    from concourse.bass_utils import run_bass_kernel_spmd

    nc = bacc.Bacc("TRN2", target_bir_lowering=False, num_devices=1)
    arrays = {f"in_{n}": a for n, a in lay_out(inputs).items()}
    io = {n[3:]: nc.dram_tensor(n, a.shape, mybir.dt.from_np(a.dtype), kind="ExternalInput").ap()
          for n, a in arrays.items()}
    out = nc.dram_tensor("y", (ROWS, P, KL, D), F32, kind="ExternalOutput").ap()
    decoder_block(nc, io, out)
    r = run_bass_kernel_spmd(nc, [arrays], core_ids=[0])
    y = r.results[0]["y"]
    return np.ascontiguousarray(y.transpose(0, 2, 1, 3).reshape(ROWS, L, D))
```

```python
from contextlib import ExitStack

import numpy as np

import concourse.bass as bass
from concourse import mybir

F32 = mybir.dt.float32
BF16 = mybir.dt.bfloat16
ALU = mybir.AluOpType
ACT = mybir.ActivationFunctionType
AX_X = mybir.AxisListType.X

P = 128
ROWS, L, D = 8, 256, 256
LAYERS, DI, S, R, TAPS = 2, 512, 64, 16, 4
E, HID = 8, 1024
KD = D // P
KI = DI // P
KL = L // P
KH = HID // P
BANK = 512
HALF = S // 2
EPS = 1e-5
CG = 4
NA, NH, NHC = 3, 3, 5
NW = 2
PE_NS = 4 / 1.2
CREDIT = 2800.0
LEAST = 700.0
GATHER = 1
DT0 = S
ONE = DT0 + R


class Token:

    def __init__(self, sem, value):
        self.sem, self.value = sem, value


class Buffer:

    def __init__(self, ap):
        self.ap, self.filled, self.read = ap, [], []

    def fill(self, *tokens):
        self.filled, self.read = list(tokens), []


class Queues:

    def __init__(self, nc, ctx):
        self.nc, self.ctx = nc, ctx
        self.queue = {e: [] for e in ("sync", "gpsimd", "scalar", "vector", "tensor")}
        self.sems, self.count, self.owner = {}, {}, {}

    def put(self, engine, stage, make, *waits, step=1):
        if stage is None:
            self.queue[engine].append((waits, make, None, 0))
            return None
        if stage not in self.sems:
            self.sems[stage] = self.ctx.enter_context(self.nc.semaphore(stage))
            self.count[stage], self.owner[stage] = 0, engine
        assert self.owner[stage] == engine
        self.count[stage] += step
        self.queue[engine].append((waits, make, self.sems[stage], step))
        return Token(self.sems[stage], self.count[stage])

    def run(self, engine, eng):
        seen = {}
        for waits, make, sem, step in self.queue[engine]:
            need = {}
            for w in waits:
                if w.value > max(seen.get(w.sem, 0), need.get(w.sem, 0)):
                    need[w.sem] = w.value
            for s, v in need.items():
                eng.wait_ge(s, v)
                seen[s] = v
            made = make(eng)
            if sem is not None:
                made.then_inc(sem, step)


def decoder_block(nc, io, out):
    ctx = ExitStack()
    with ctx:
        q = Queues(nc, ctx)
        put = q.put

        def sb(name, shape, dt=F32):
            return ctx.enter_context(nc.sbuf_tensor(name, shape, dt))

        def psum(name, shape):
            return ctx.enter_context(nc.psum_tensor(name, shape, F32))

        psY = psum("psY", [P, KL, DI])
        psU = [psum(f"psU{i}", [P, KI // 2, L]) for i in range(2)]
        psB = [psum(f"psB{i}", [P, BANK]) for i in range(2)]
        psG = [psum(f"psG{i}", [P, BANK]) for i in range(2)]
        dtuB = [Buffer(x) for x in psU]
        ysum = Buffer(psY)
        bbank = [Buffer(x) for x in psB]
        bank = [Buffer(x) for x in psG]

        w_in = sb("w_in", [P, LAYERS, KD, 2 * DI])
        w_x = sb("w_x", [P, LAYERS, KI, 6 * HALF + S + R])
        w_dt = sb("w_dt", [P, LAYERS, DI])
        w_out = sb("w_out", [P, LAYERS, KI, D])
        negA = sb("negA", [P, LAYERS, KI, S])
        conv_w = sb("conv_w", [P, LAYERS, KI, TAPS + 1])
        dskip = sb("dskip", [P, LAYERS, KI])
        diagD = sb("diagD", [P, LAYERS, KI, P])
        w_att = sb("w_att", [P, 4, KD, D])
        b_att = sb("b_att", [P, 2, KD])
        bo_row = sb("bo_row", [1, D])
        w_gate = sb("w_gate", [P, KD, E])
        b1 = sb("b1", [P, E, KH])
        b2 = sb("b2", [E, D])
        ident = sb("ident", [P, P])
        sel = sb("sel", [3 * HALF, HALF, P], BF16)
        ones_row = sb("ones_row", [1, P])
        neg_half = sb("neg_half", [P, KL])
        rank = sb("rank", [P, KL, E])

        xin = [Buffer(sb(f"xin{i}", [P, KD, L])) for i in range(4)]
        scratch = Buffer(sb("scratch", [P, KI, L]))
        u = [Buffer(sb(f"u{i}", [P, KI, L])) for i in range(2)]
        sz = [Buffer(sb(f"sz{i}", [P, KL, DI])) for i in range(2)]
        dt = [Buffer(sb(f"dt{i}", [P, KI, L])) for i in range(2)]
        dtu = [Buffer(sb(f"dtu{i}", [P, KI, L])) for i in range(2)]
        cdt = Buffer(sb("cdt", [P, L]))
        bparts = [Buffer(sb(f"bparts{i}", [3 * HALF, 2, L], BF16)) for i in range(2)]
        brest = Buffer(sb("brest", [3 * HALF, 2, L]))
        bmid = Buffer(sb("bmid", [3 * HALF, 2, L], BF16))
        dA = [Buffer(sb(f"dA{i}", [P, KI, L])) for i in range(NA)]
        h = [Buffer(sb(f"h{i}", [P, KI, L])) for i in range(NH)]
        hC = [Buffer(sb(f"hC{i}", [P, KI, L])) for i in range(NHC)]
        cb = [Buffer(sb(f"cb{i}", [P, CG, L])) for i in range(2)]
        gT = Buffer(sb("gT", [P, KL, DI]))
        tapped = [Buffer(gT.ap[:, i, :].rearrange("p (c t) -> p c t", c=2)) for i in range(2)]
        g = scratch
        c_dram = [Buffer(nc.dram_tensor(f"c_dram{i}", [S, L], F32, kind="Internal").ap()) for i in range(2)]

        xrow = Buffer(sb("xrow", [P, KL, D]))
        ctxT = Buffer(sb("ctxT", [P, KD, L]))
        resid = Buffer(sb("resid", [P, KL, D]))
        x1 = Buffer(sb("x1", [P, KL, D]))
        x1T = Buffer(sb("x1T", [P, KD, L]))
        qT = Buffer(sb("qT", [P, KD, L]))
        kT = Buffer(sb("kT", [P, KD, L]))
        vv = Buffer(sb("vv", [P, KL, D]))
        prob = Buffer(sb("prob", [P, KL, L]))
        x2 = Buffer(sb("x2", [P, KL, D]))
        x2T = x1T
        hid = [kT, vv]
        wexp = [Buffer(sb(f"wexp{i}", [P, 2 * HID])) for i in range(NW)]
        acc = x2
        fin = resid
        small = sb("small", [P, 64])
        stats = sb("stats", [P, KL, 6])
        gl = sb("gl", [P, 8, KL, E])
        combT = Buffer(sb("combT", [E, L]))

        loads = []

        def load(dst, name, queue="sync"):
            return put(queue, "weights_in" if queue == "sync" else "weights_in2",
                       lambda e: e.dma_start(dst, io[name]), step=16)

        def load_row(b):
            x = xin[b % 2]
            x.fill(put("sync", f"xT_in{b % 2}", lambda e: e.dma_start(x.ap[:, :, :], io["xT"][b]), *x.read, step=16))

        load_row(0)
        loads.append(load(w_in[:, :, :, :], "w_in"))
        w_in_ready = loads[-1]
        loads.append(load(conv_w[:, :, :, :], "conv"))
        loads.append(load(w_x[:, :, :, :], "w_x"))
        loads.append(load(w_dt[DT0:ONE + 1, :, :], "w_dt"))
        loads.append(load(negA[:, :, :, :], "A_log", "scalar"))
        a_in = loads[-1]
        loads.append(load(dskip[:, :, :], "D_skip", "scalar"))
        skip_in = loads[-1]
        loads.append(load(w_out[:, :, :, :], "w_out", "scalar"))
        loads.append(load(w_att[:, :, :, :], "w_att", "scalar"))
        loads.append(load(b_att[:, :, :], "b_att", "scalar"))
        loads.append(load(bo_row[:, :], "bo", "scalar"))
        loads.append(load(w_gate[:, :, :], "w_gate", "scalar"))
        loads.append(load(b1[:, :, :], "b1", "scalar"))
        loads.append(load(b2[:, :], "b2", "scalar"))
        w_ready = [[t for t in loads if t.sem is s][-1] for s in (w_in_ready.sem, a_in.sem)]
        w_in_ready = w_ready[0]

        done = []

        def pool(make, *waits):
            done.append(put("gpsimd", "setup", make, *waits, *done[-1:]))

        pool(lambda e: e.memset(ident[:, :], 0.0))
        pool(lambda e: e.affine_select(
            out=ident[:, :], in_=ident[:, :], compare_op=ALU.not_equal, fill=1.0, base=0,
            pattern=[[-1, P]], channel_multiplier=1))
        pool(lambda e: e.memset(sel[:, :, :], 0.0))
        for part in range(3):
            pool(lambda e, part=part: e.affine_select(
                out=sel[:, :, :], in_=sel[:, :, :], compare_op=ALU.not_equal, fill=1.0,
                base=-HALF * part, pattern=[[-1, HALF], [0, P]], channel_multiplier=1))
        pool(lambda e: e.memset(ones_row[:, :], 1.0))
        pool(lambda e: e.memset(neg_half[:, :], -0.5))
        pool(lambda e: e.memset(cdt.ap[DT0:DT0 + 32, :], 1.0))
        for i in range(E):
            pool(lambda e, i=i: e.memset(rank[:, :, i:i + 1], float(E - i)))
        for a in dA:
            pool(lambda e, a=a: e.memset(a.ap[:, :, 0:1], 0.0))
        for l in range(LAYERS):
            for c in range(KI):
                pool(lambda e, l=l, c=c: e.tensor_scalar(
                    diagD[:, l, c, :], ident[:, :], dskip[:, l, c:c + 1], None, ALU.mult), w_ready[1])
        setup = done[-1]
        cdt.fill(setup)
        put("scalar", None, lambda e: e.preload_act_table_set("natural_log_exp_and_others"))
        expA = put("scalar", "expA", lambda e: e.activation(
            negA[:, :, :, :], negA[:, :, :, :], ACT.Exp), w_ready[1])
        A_ready = put("vector", "negA", lambda e: e.tensor_scalar(
            negA[:, :, :, :], negA[:, :, :, :], -1.0, None, ALU.mult), expA)


        pe_time = [0.0]

        def mm(stage, dst, pairs, *waits, start=True, check=False):
            n = len(pairs)
            pe_time[0] += n * PE_NS * pairs[0][1].shape[-1]
            for i, (lhs, rhs) in enumerate(pairs):
                t = put("tensor", stage if i == n - 1 else None,
                        lambda e, lhs=lhs, rhs=rhs, i=i: e.matmul(
                            dst, lhs, rhs, start=start and i == 0, stop=i == n - 1,
                            skip_group_check=check), *(waits if i == 0 else ()))
            return t

        def transpose(stage, dst, src, *waits):
            pe_time[0] += P * PE_NS / 4
            return put("tensor", stage, lambda e: e.transpose(dst, src, ident[:, :]), *waits)

        def act(stage, dst, src, func, *waits, **kw):
            return put("scalar", stage, lambda e: e.activation(dst, src, func, **kw), *waits)

        def pre(l, n, x):
            su, ssz, sdt, sdtu, sbp = u[n % 2], sz[n % 2], dt[n % 2], dtu[n % 2], bparts[n % 2]

            def taps(half, t):
                k, w = bank[half], None
                for j in range(TAPS):
                    dst = scratch if j == 0 else tapped[j % 2]
                    for i in range(2):
                        c = 2 * half + i
                        at = dst.ap[:, c, :] if j == 0 else dst.ap[:, i, :]
                        m = act("conv", at, k.ap[:, i * L:(i + 1) * L], ACT.Identity, t, *dst.read,
                                scale=conv_w[:, l, c, TAPS - 1 - j:TAPS - j],
                                **({"bias": conv_w[:, l, c, TAPS:TAPS + 1]} if j == 0 else {}))
                    if j == 0:
                        w = m
                        continue
                    w = put("gpsimd", "conv_add", lambda e, j=j, dst=dst: e.tensor_tensor(
                        scratch.ap[:, 2 * half:2 * half + 2, j:], scratch.ap[:, 2 * half:2 * half + 2, j:],
                        dst.ap[:, :, :L - j], ALU.add), m, w)
                    dst.read = [w]
                k.read = [m]
                return [w]

            for x_ in tapped:
                x_.read = list(gT.read)
            zs = []
            for tc in range(KL):
                k = bank[tc]
                t = mm("in_proj", k.ap[:, :], [(x.ap[:, d, tc * P:(tc + 1) * P], w_in[:, l, d, DI:2 * DI])
                                               for d in range(KD)], *x.filled, *k.read, *w_ready)
                yield
                s = act("z", ssz.ap[:, tc, :], k.ap[:, :], ACT.Copy, t, *ssz.read)
                k.read = [s]
                zs.append(s)
            ts = []
            for half in range(2):
                k = bank[half]
                for i in range(2):
                    c = 2 * half + i
                    t = mm("in_proj", k.ap[:, i * L:(i + 1) * L],
                           [(w_in[:, l, d, c * P:(c + 1) * P], x.ap[:, d, :]) for d in range(KD)], *k.read)
                ts.append(t)
                yield
                if half == 0:
                    v = taps(0, t)
            x.read = [t]
            v += taps(1, t)
            gT.read = [y for x_ in tapped for y in x_.read]
            yield
            s1 = act("silu", ssz.ap[:, :, :], ssz.ap[:, :, :], ACT.Silu, *zs)
            ssz.fill(s1)
            s = act("silu", su.ap[:, :, :], scratch.ap[:, :, :], ACT.Silu, *v, *su.read)
            su.fill(s)
            scratch.fill(*v)
            scratch.read = [s]
            put("scalar", None, lambda e: e.preload_act_table_set("natural_log_exp_and_others"))
            yield
            kb, kc = bank
            for half in range(2):
                t = mm("x_proj", kb.ap[0:3 * HALF, half * L:(half + 1) * L],
                       [(w_x[:, l, c, half * 3 * HALF:(half + 1) * 3 * HALF], su.ap[:, c, :]) for c in range(KI)],
                       s, *kb.read)
                yield
            tc_ = mm("x_proj", kc.ap[0:S + R, 0:L], [(w_x[:, l, c, 6 * HALF:6 * HALF + S + R], su.ap[:, c, :])
                                                     for c in range(KI)], *kc.read)
            su.read = [tc_]
            b3 = kb.ap[0:3 * HALF, :].rearrange("p (a t) -> p a t", a=2)
            hi = act("b_hi", sbp.ap[:, :, :], b3, ACT.Copy, t, *sbp.read)
            yield
            cs = act("c_dt", cdt.ap[0:S + R, :], kc.ap[0:S + R, 0:L], ACT.Copy, tc_, *cdt.read, *cdt.filled)
            kc.read = [cs]
            cdt.fill(cs)
            r1 = put("vector", "b_rest", lambda e: e.tensor_tensor(brest.ap[:, :, :], b3, sbp.ap[:, :, :],
                                                                   ALU.subtract), hi, *brest.read)
            kb.read = [r1]
            cd = c_dram[n % 2]
            cd.fill(put("sync", "c_out", lambda e: e.dma_start(cd.ap, cdt.ap[0:S, :]), cs, *cd.read, step=16))
            yield
            mid = act("b_mid", bmid.ap[:, :, :], brest.ap[:, :, :], ACT.Copy, r1, *bmid.read)
            dts = []
            for half in range(2):
                k = bank[half]
                for i in range(2):
                    c = 2 * half + i
                    t = mm("dt_proj", k.ap[:, i * L:(i + 1) * L],
                           [(w_dt[DT0:ONE + 1, l, c * P:(c + 1) * P], cdt.ap[DT0:ONE + 1, :])], cs, *k.read)
                dts.append(t)
            cdt.read = [cd.filled[0], t]
            yield
            r2 = put("gpsimd", "b_rest2", lambda e: e.tensor_tensor(brest.ap[:, :, :], brest.ap[:, :, :],
                                                                   bmid.ap[:, :, :], ALU.subtract), mid, r1)
            ab = [act("softplus", scratch.ap[:, 2 * i:2 * i + 2, :],
                      bank[i].ap[:, :].rearrange("p (a t) -> p a t", a=2), ACT.Abs, dts[i], *scratch.read)
                  for i in range(2)]
            ex = act("softplus", scratch.ap[:, :, :], scratch.ap[:, :, :], ACT.Exp, *ab, scale=-1.0)
            yield
            ln = act("softplus", scratch.ap[:, :, :], scratch.ap[:, :, :], ACT.Ln, ex, bias=1.0)
            m1 = act("b_lo", sbp.ap[HALF:2 * HALF, :, :], bmid.ap[HALF:2 * HALF, :, :], ACT.Copy, r2, hi)
            m2 = act("b_lo", sbp.ap[2 * HALF:3 * HALF, :, :], brest.ap[2 * HALF:3 * HALF, :, :], ACT.Copy, r2, r1)
            bmid.read, brest.read = [m1], [m2]
            sbp.fill(m2)
            yield
            for i in range(2):
                src = bank[i].ap[:, :].rearrange("p (a t) -> p a t", a=2)
                v = put("vector", "dt", lambda e, i=i, src=src: e.scalar_tensor_tensor(
                    out=sdt.ap[:, 2 * i:2 * i + 2, :], in0=src, scalar=0.0, in1=scratch.ap[:, 2 * i:2 * i + 2, :],
                    op0=ALU.max, op1=ALU.add), ln, *sdt.read)
                bank[i].read = [v]
            scratch.fill(ln)
            scratch.read = [v]
            sdt.fill(v)
            yield
            w = put("gpsimd", "dtu", lambda e: e.tensor_tensor(sdtu.ap[:, :, :], sdt.ap[:, :, :], su.ap[:, :, :],
                                                               ALU.mult), v, s, *sdtu.read)
            sdtu.fill(w)
            su.read.append(w)
            yield

        def gate_and_turn(l, n):
            su, ssz = u[n % 2], sz[n % 2]
            toks = []
            for tc in range(KL):
                for c in range(KI):
                    t = put("tensor", "y_done", lambda e, tc=tc, c=c: e.matmul(
                        psY[:, tc, c * P:(c + 1) * P], su.ap[:, c, tc * P:(tc + 1) * P], diagD[:, l, c, :],
                        start=False, stop=True, skip_group_check=True), *su.filled, setup)
                toks.append(put("vector", "gate", lambda e, tc=tc: e.tensor_tensor(
                    gT.ap[:, tc, :], psY[:, tc, :], ssz.ap[:, tc, :], ALU.mult), t, *ssz.filled, *gT.read))
            su.read.append(t)
            ysum.read = [toks[-1]]
            gT.fill(*toks)
            ssz.read = [toks[-1]]

        def turned():
            outs = []
            for half in range(2):
                k = bank[half]
                for i in range(2):
                    for tc in range(KL):
                        c = 2 * half + i
                        t = transpose("g_turn", k.ap[:, i * L + tc * P:i * L + (tc + 1) * P],
                                      gT.ap[:, tc, c * P:(c + 1) * P], *gT.filled, *k.read, setup)
                yield
                s = act("g", g.ap[:, 2 * half:2 * half + 2, :], k.ap[:, :].rearrange("p (a t) -> p a t", a=2),
                        ACT.Copy, t, *g.read)
                k.read = [s]
                outs.append(s)
            gT.read = [t]
            g.fill(*outs)
            yield

        def post_inner(l, n, nxt):
            yield from turned()
            k = bank[0]
            for i in range(KD):
                t = mm("out_proj", k.ap[:, i * L:(i + 1) * L],
                       [(w_out[:, l, c, i * P:(i + 1) * P], g.ap[:, c, :]) for c in range(KI)], *g.filled, *k.read)
                yield
            g.read = [t]
            s = act("x_next", nxt.ap[:, :, :], k.ap[:, :].rearrange("p (a t) -> p a t", a=2), ACT.Copy, t, *nxt.read)
            k.read = [s]
            nxt.fill(s)
            yield

        def layernorm(src, dst, where, *waits):
            mv = small[:, where:where + 4].rearrange("p (c s) -> p c s", c=KL)
            rs = small[:, where + 4:where + 6]
            toks = []
            for tc in range(KL):
                v = put("vector", "norm", lambda e, tc=tc: e.bn_stats(stats[:, tc, :], src.ap[:, tc, :]),
                        *waits, *src.filled)
                toks.append(put("vector", "norm", lambda e, tc=tc: e.bn_aggr(mv[:, tc, :], stats[:, tc, :]), v))
            v = put("vector", "norm", lambda e: e.tensor_scalar(mv[:, :, 1], mv[:, :, 1], EPS, None, ALU.add), *toks)
            yield
            p = put("gpsimd", "rstd", lambda e: e.tensor_tensor(rs, mv[:, :, 1], neg_half[:, :], ALU.pow), v, setup)
            yield
            for tc in range(KL):
                v = put("vector", "norm", lambda e, tc=tc: e.tensor_scalar(
                    dst.ap[:, tc, :], src.ap[:, tc, :], mv[:, tc, 0:1], rs[:, tc:tc + 1], ALU.subtract, ALU.mult),
                    p, *dst.read)
            dst.fill(v)
            src.read = [v]

        def load_ctx(b):
            ctxT.fill(put("sync", "ctx_in", lambda e: e.dma_start(ctxT.ap[:, :, :], io["ctxT"][b]), *ctxT.read, step=16))
            xrow.fill(put("sync", "xrow_in", lambda e: e.dma_start(xrow.ap[:, :, :], io["x"][b]), *xrow.read, step=16))

        def post_outer(l, b):
            load_ctx(b)
            yield from turned()
            k = bank[0]
            for tc in range(KL):
                t = mm("out_proj", k.ap[:, tc * D:(tc + 1) * D],
                       [(g.ap[:, c, tc * P:(tc + 1) * P], w_out[:, l, c, :]) for c in range(KI)], *g.filled, *k.read)
                yield
            g.read = [t]
            v = put("vector", "resid", lambda e: e.tensor_tensor(
                resid.ap[:, :, :], k.ap[:, :].rearrange("p (a t) -> p a t", a=2), xrow.ap[:, :, :], ALU.add),
                t, *xrow.filled, *resid.read)
            k.read = [v]
            xrow.read = [v]
            resid.fill(v)
            yield from layernorm(resid, x1, 0)
            yield

        def turn_rows(stage, src, dst, k):
            for d in range(KD):
                for tc in range(KL):
                    t = transpose(stage, k.ap[:, d * L + tc * P:d * L + (tc + 1) * P],
                                  src.ap[:, tc, d * P:(d + 1) * P], *src.filled, *k.read, setup)
            src.read.append(t)
            yield
            s = act("turned", dst.ap[:, :, :], k.ap[:, :].rearrange("p (a t) -> p a t", a=2), ACT.Copy, t, *dst.read)
            k.read = [s]
            dst.fill(s)
            yield

        def attention(b):
            WQ, WK, WV, WO = range(4)
            two = lambda k: k.ap[:, :].rearrange("p (a t) -> p a t", a=2)
            k0, k1 = bank
            for i in range(KD):
                tk = mm("attn", k1.ap[:, i * L:(i + 1) * L],
                        [(w_att[:, WK, d, i * P:(i + 1) * P], ctxT.ap[:, d, :]) for d in range(KD)],
                        *ctxT.filled, *k1.read, *w_ready)
            yield
            s = act("kv", kT.ap[:, :, :], two(k1), ACT.Copy, tk, *kT.read)
            k1.read = [s]
            kT.fill(s)
            for tc in range(KL):
                t = mm("attn", k0.ap[:, tc * D:(tc + 1) * D],
                       [(ctxT.ap[:, d, tc * P:(tc + 1) * P], w_att[:, WV, d, :]) for d in range(KD)], *k0.read)
            ctxT.read = [t]
            yield
            s = act("kv", vv.ap[:, :, :], two(k0), ACT.Copy, t, *vv.read)
            k0.read = [s]
            vv.fill(s)
            yield from turn_rows("attn", x1, x1T, k1)
            for i in range(KD):
                t = mm("attn", k0.ap[:, i * L:(i + 1) * L],
                       [(w_att[:, WQ, d, i * P:(i + 1) * P], x1T.ap[:, d, :]) for d in range(KD)],
                       *x1T.filled, *k0.read)
            x1T.read = [t]
            yield
            for i in range(KD):
                s = act("q", qT.ap[:, i, :], k0.ap[:, i * L:(i + 1) * L], ACT.Identity, t, *qT.read,
                        bias=b_att[:, 0, i:i + 1])
            k0.read = [s]
            qT.fill(s)
            yield
            scale = float(D) ** -0.5
            for tc in range(KL):
                t = mm("attn", k1.ap[:, tc * L:(tc + 1) * L],
                       [(qT.ap[:, d, tc * P:(tc + 1) * P], kT.ap[:, d, :]) for d in range(KD)],
                       *qT.filled, *kT.filled, *k1.read)
            qT.read, kT.read = [t], [t]
            yield
            mx, nm, rsum, rinv = (small[:, 8 + 2 * i:10 + 2 * i] for i in range(4))
            v = put("vector", "softmax", lambda e: e.tensor_reduce(mx, two(k1), AX_X, ALU.max), t)
            v = put("vector", "softmax", lambda e: e.tensor_scalar(nm, mx, -scale, None, ALU.mult), v)
            yield
            for tc in range(KL):
                s = act("prob", prob.ap[:, tc, :], k1.ap[:, tc * L:(tc + 1) * L], ACT.Exp, v, *prob.read,
                        scale=scale, bias=nm[:, tc:tc + 1], accum_out=rsum[:, tc:tc + 1])
            k1.read = [s]
            yield
            v = put("vector", "softmax", lambda e: e.reciprocal(rinv, rsum), s)
            for tc in range(KL):
                w = put("vector", "softmax", lambda e, tc=tc: e.tensor_scalar(
                    prob.ap[:, tc, :], prob.ap[:, tc, :], rinv[:, tc:tc + 1], None, ALU.mult), v)
            prob.fill(w)
            yield
            for kc in range(KL):
                for tc in range(KL):
                    t = transpose("attn", k0.ap[:, kc * L + tc * P:kc * L + (tc + 1) * P],
                                  prob.ap[:, tc, kc * P:(kc + 1) * P], *prob.filled, *k0.read)
            prob.read = [t]
            yield
            s = act("turned", x1T.ap[:, :, :], two(k0), ACT.Copy, t, *x1T.read)
            k0.read = [s]
            x1T.fill(s)
            yield
            for i in range(KD):
                t = mm("attn", k1.ap[:, i * L:(i + 1) * L],
                       [(vv.ap[:, kc, i * P:(i + 1) * P], x1T.ap[:, kc, :]) for kc in range(KL)],
                       *x1T.filled, *vv.filled, *k1.read)
            vv.read = [t]
            x1T.read = [t]
            yield
            for i in range(KD):
                s = act("q", qT.ap[:, i, :], k1.ap[:, i * L:(i + 1) * L], ACT.Identity, t, *qT.read,
                        bias=b_att[:, 1, i:i + 1])
            k1.read = [s]
            qT.fill(s)
            yield
            for tc in range(KL):
                t = mm("attn", k0.ap[:, tc * D:(tc + 1) * D],
                       [(qT.ap[:, d, tc * P:(tc + 1) * P], w_att[:, WO, d, :]) for d in range(KD)]
                       + [(ones_row[:, :], bo_row[:, :])], *qT.filled, *k0.read)
            qT.read = [t]
            yield
            v = put("vector", "resid", lambda e: e.tensor_tensor(
                resid.ap[:, :, :], two(k0), x1.ap[:, :, :], ALU.add), t, *x1.filled, *resid.read)
            k0.read = [v]
            x1.read.append(v)
            resid.fill(v)
            yield from layernorm(resid, x2, 16)
            yield

        def route(b):
            yield from turn_rows("moe_turn", x2, x2T, bank[1])
            k = bank[0]
            for tc in range(KL):
                t = mm("gate_mm", k.ap[:, tc * E:(tc + 1) * E],
                       [(x2T.ap[:, d, tc * P:(tc + 1) * P], w_gate[:, d, :]) for d in range(KD)],
                       *x2T.filled, *k.read)
            x2T.read = [t]
            yield
            lg = k.ap[:, 0:KL * E].rearrange("p (c e) -> p c e", c=KL)
            pr, w0, key, hot1, hot2, hot = (gl[:, i, :, :] for i in range(6))
            m = lambda i: small[:, 24 + 2 * i:26 + 2 * i]
            wide = lambda x: x.rearrange("p (c e) -> p c e", e=1).to_broadcast([P, KL, E])

            def v(make, *waits):
                v.last = put("vector", "route", make, *waits, *([v.last] if v.last else []))
                return v.last

            v.last = None
            v(lambda e: e.tensor_reduce(m(0), lg, AX_X, ALU.max), t, *combT.read)
            a = v(lambda e: e.tensor_tensor(w0, lg, wide(m(0)), ALU.subtract))
            k.read = [a]
            yield
            s = act("route_exp", pr, w0, ACT.Exp, a)
            yield
            v(lambda e: e.tensor_reduce(m(1), pr, AX_X, ALU.add), s)
            v(lambda e: e.reciprocal(m(2), m(1)))
            v(lambda e: e.tensor_tensor(pr, pr, wide(m(2)), ALU.mult))
            yield
            src = pr
            for hotn, mi in ((hot1, 3), (hot2, 4)):
                v(lambda e, src=src, mi=mi: e.tensor_reduce(m(mi), src, AX_X, ALU.max))
                v(lambda e, src=src, mi=mi: e.tensor_tensor(key, src, wide(m(mi)), ALU.is_equal))
                v(lambda e: e.tensor_tensor(key, key, rank[:, :, :], ALU.mult))
                v(lambda e: e.tensor_reduce(m(5), key, AX_X, ALU.max))
                v(lambda e, hotn=hotn: e.tensor_tensor(hotn, key, wide(m(5)), ALU.is_equal))
                if src is pr:
                    v(lambda e: e.scalar_tensor_tensor(out=w0, in0=hot1, scalar=-2.0, in1=pr,
                                                       op0=ALU.mult, op1=ALU.add))
                    src = w0
                yield
            v(lambda e: e.tensor_tensor(hot, hot1, hot2, ALU.add))
            v(lambda e: e.tensor_tensor(hot, hot, pr, ALU.mult))
            v(lambda e: e.tensor_tensor(m(6), m(3), m(4), ALU.add))
            v(lambda e: e.reciprocal(m(7), m(6)))
            a = v(lambda e: e.tensor_tensor(hot, hot, wide(m(7)), ALU.mult), *acc.read)
            yield
            k = bank[1]
            for tc in range(KL):
                t = put("tensor", "moe_turn", lambda e, tc=tc, k=k: e.transpose(
                    k.ap[0:E, tc * P:(tc + 1) * P], hot[:, tc, :], ident[:, :]), a, *k.read)
            yield
            s = act("combT", combT.ap[:, :], k.ap[0:E, 0:L], ACT.Copy, t, *combT.read)
            combT.fill(s)
            k.read = [s]
            yield
            k = bank[0]
            for tc in range(KL):
                t = mm("gate_mm", k.ap[:, tc * D:(tc + 1) * D],
                       [(combT.ap[:, tc * P:(tc + 1) * P], b2[:, :])], s, *k.read)
            combT.read = [t]
            yield
            w = put("vector", "acc", lambda e: e.tensor_tensor(
                acc.ap[:, :, :], bank[0].ap[:, :].rearrange("p (a t) -> p a t", a=2), x2.ap[:, :, :], ALU.add),
                t, *x2.filled, *x2.read)
            k.read = [w]
            acc.fill(w)
            yield

        def load_half(b, e, half):
            n = (b * E + e) * 2 + half
            w = wexp[n % NW]
            w.fill(put("sync", f"wexp_in{n % NW}", lambda en: en.dma_start(w.ap[:, :], io["w_exp"][e, half]),
                       *w.read, step=16))

        halves = [(b, e, f) for b in range(ROWS) for e in range(E) for f in range(2)]

        def experts(b, which):
            hot = gl[:, 5, :, :]
            HB, OB = bank[0], bank[1]
            late = []

            def fetch(at):
                if at < len(halves):
                    load_half(*halves[at])

            def add_up(e, t):
                for tc in range(KL):
                    v = put("vector", "acc", lambda en, tc=tc: en.scalar_tensor_tensor(
                        out=acc.ap[:, tc, :], in0=OB.ap[:, tc * D:(tc + 1) * D], scalar=hot[:, tc, e:e + 1],
                        in1=acc.ap[:, tc, :], op0=ALU.mult, op1=ALU.add), t, *acc.filled)
                OB.read = [v]
                acc.fill(v)

            for e in which:
                pending = []
                first = True

                def out_pair():
                    nonlocal first
                    w, j, hb, last = pending.pop(0)
                    pe_time[0] += 2 * KL * D * PE_NS
                    for i in range(2):
                        for tc in range(KL):
                            t = put("tensor", "moe_out", lambda en, i=i, tc=tc, st=first: en.matmul(
                                OB.ap[:, tc * D:(tc + 1) * D], hb.ap[:, i, tc * P:(tc + 1) * P],
                                w.ap[:, HID + (j + i) * D:HID + (j + i + 1) * D], start=st, stop=last,
                                skip_group_check=True), *hb.filled, *(OB.read if first else ()))
                            first = False
                    hb.read = [t]
                    w.read = [t]
                    return t

                for pair in range(KH // 2):
                    half, j = pair // 2, 2 * (pair % 2)
                    w = wexp[((b * E + e) * 2 + half) % NW]
                    w1 = w.ap[:, 0:HID].rearrange("p (k m) -> p k m", k=KD)
                    hb = hid[pair % 2]
                    for i in range(2):
                        t = mm("moe_hid", HB.ap[:, i * L:(i + 1) * L],
                               [(w1[:, d, (j + i) * P:(j + i + 1) * P], x2T.ap[:, d, :]) for d in range(KD)],
                               *w.filled, *HB.read)
                    if pair == 0 and late:
                        add_up(*late.pop())
                    yield
                    for i in range(2):
                        c = 2 * pair + i
                        s = act("moe_relu", hb.ap[:, i, :], HB.ap[:, i * L:(i + 1) * L], ACT.Relu, t, *hb.read,
                                bias=b1[:, e, c:c + 1])
                    hb.fill(s)
                    HB.read = [s]
                    pending.append((w, j, hb, pair == KH // 2 - 1))
                    if pair > 0:
                        out_pair()
                        if pair == 2:
                            fetch((b * E + e) * 2 + NW)
                        yield
                x2T.read.append(t)
                if e + 1 not in which:
                    yield
                t = out_pair()
                fetch((b * E + e) * 2 + 1 + NW)
                late.append((e, t))
                yield
            add_up(*late.pop())
            yield

        def finish(b):
            yield from layernorm(acc, fin, 40)
            o = put("sync", "out", lambda e: e.dma_start(out[b], fin.ap[:, :, :]), *fin.filled, step=16)
            fin.read = [o]
            yield


        jobs = [(0, 0)]
        for b in range(1, ROWS):
            jobs += [(0, b), (1, b - 1)]
        jobs.append((1, ROWS - 1))
        STEPS = len(jobs) * S

        def step_decay(i):
            (l, _), n, s = jobs[i // S], i // S, i % S
            a, sdt = dA[i % NA], dt[n % 2]
            for c in range(KI):
                t = act("dA", a.ap[:, c, 1:L], sdt.ap[:, c, 1:L], ACT.Exp, *sdt.filled, *a.read, A_ready, setup,
                        scale=negA[:, l, c, s:s + 1])
            a.fill(t)
            if s == S - 1:
                sdt.read = [t]

        def step_scan(i):
            n = i // S
            sdtu, kb, a, hh = dtu[n % 2], bbank[(i // 2) % 2], dA[i % NA], h[i % NH]
            wide = kb.ap[:, (i % 2) * L:(i % 2 + 1) * L].rearrange("p (a t) -> p a t", a=1).to_broadcast([P, 2, L])
            ms, rs = [], []
            for f in range(2):
                m = put("vector", "dtuB", lambda e, f=f: e.tensor_tensor(
                    psU[f][:, :, :], sdtu.ap[:, 2 * f:2 * f + 2, :], wide, ALU.mult),
                    *kb.filled, *sdtu.filled, *dtuB[f].read)
                ms.append(m)
            for f in range(2):
                flat = lambda x, f=f: x[:, 2 * f:2 * f + 2, :].rearrange("p c t -> p (c t)")
                r = put("vector", "scan", lambda e, f=f, flat=flat: e.tensor_tensor_scan(
                    flat(hh.ap), flat(a.ap), psU[f].rearrange("p c t -> p (c t)"), 0.0, ALU.mult, ALU.add),
                    *a.filled, ms[f], *hh.read)
                dtuB[f].read = [r]
                rs.append(r)
            kb.read, a.read = [m], [r]
            hh.fill(*rs)
            if i % S == S - 1:
                sdtu.read = [m]

        def step_out(i):
            hh, hc, kc = h[i % NH], hC[i % NHC], cb[(i // CG) % 2]
            cw = kc.ap[:, i % CG:i % CG + 1, :]
            p = put("gpsimd", "hC", lambda e: e.tensor_tensor(
                hc.ap[:, :, :], hh.ap[:, :, :], cw.to_broadcast([P, KI, L]), ALU.mult),
                *hh.filled, *kc.filled, *hc.read)
            hh.read = [p]
            kc.read = [p]
            hc.fill(p)

        def step_sum(i):
            hc, s = hC[i % NHC], i % S
            for tc in range(KL):
                for c in range(KI):
                    x = put("tensor", "y_sum" if (tc, c) == (KL - 1, KI - 1) else None,
                            lambda e, tc=tc, c=c: e.matmul(
                                psY[:, tc, c * P:(c + 1) * P], hc.ap[:, c, tc * P:(tc + 1) * P], ident[:, :],
                                start=s == 0 and c == 0, stop=False, is_transpose=True,
                                skip_group_check=True), *hc.filled, *(ysum.read if s == 0 else ()), setup)
            hc.read = [x]

        def spread_b(pair):
            n = 2 * pair // S
            k, sbp = bbank[pair % 2], bparts[n % 2]
            for j in range(2):
                s = (2 * pair + j) % S
                t = put("tensor", "b_wide", lambda e, s=s, j=j: e.matmul(
                    k.ap[:, j * L:(j + 1) * L], sel[:, s % HALF, :], sbp.ap[:, s // HALF, :],
                    start=True, stop=True), *sbp.filled, *k.read, setup)
            k.fill(t)
            sbp.read = [t]

        def load_c(group):
            n, at = group * CG // S, group * CG % S
            k, cd = cb[group % 2], c_dram[n % 2]
            src = cd.ap[at:at + CG, :].rearrange("(a s) t -> a s t", a=1)
            k.fill(put("sync", f"c_in{group % 2}", lambda e: e.dma_start(
                k.ap[:, :, :], src.to_broadcast([P, CG, L])), *cd.filled, *k.read, step=16))
            cd.read.append(k.filled[0])


        def source(l, b):
            return xin[2 * l + b % 2]

        def urgent(n):
            if n > 0:
                pl, pb = jobs[n - 1]
                yield post_inner(pl, n - 1, source(1, pb)) if pl == 0 else post_outer(pl, pb)
            if n + 1 < len(jobs):
                nl, nb = jobs[n + 1]
                if nl == 0:
                    load_row(nb)
                yield pre(nl, n + 1, source(nl, nb))

        owed = 0.0
        first, then = [], []

        def unit():
            while True:
                if unit.now is None:
                    if not first and not then:
                        return None
                    unit.now = (first or then).pop(0)
                before = pe_time[0]
                if next(unit.now, True) is None:
                    return max(pe_time[0] - before, LEAST)
                unit.now = None

        unit.now = None

        for i in range(NW):
            load_half(*halves[i])
        for _ in pre(0, 0, xin[0]):
            pass
        load_c(0)
        load_c(1)
        spread_b(0)
        spread_b(1)
        for i in range(-2, STEPS + 1):
            if i + 2 < STEPS:
                step_decay(i + 2)
            if 0 <= i + 1 < STEPS:
                step_scan(i + 1)
                if i % 2 == 0 and (i + 1) // 2 + 2 < STEPS // 2:
                    spread_b((i + 1) // 2 + 2)
            if 0 <= i < STEPS:
                step_out(i)
                if i % CG == CG - 1 and i // CG + 2 < STEPS // CG:
                    load_c(i // CG + 2)
            if i >= 1:
                step_sum(i - 1)
                if i % S == 0:
                    n = i // S - 1
                    gate_and_turn(jobs[n][0], n)
            if 0 <= i < STEPS:
                n, s = i // S, i % S
                if s == 1:
                    if n > 0 and jobs[n - 1][0] == 1:
                        first, then = then, []
                    first += urgent(n)
                    if n > 0 and jobs[n - 1][0] == 1:
                        b = jobs[n - 1][1]
                        then += [attention(b), route(b)] + [experts(b, range(e, e + 2)) for e in range(0, E, 2)] + [finish(b)]
                if s >= 1:
                    owed = min(owed + CREDIT, 2 * CREDIT * GATHER)
                    if s % GATHER == 0:
                        while owed > 0:
                            cost = unit()
                            if cost is None:
                                break
                            owed -= cost
        b = jobs[-1][1]
        first += urgent(len(jobs))
        then += [attention(b), route(b), experts(b, range(E)), finish(b)]
        while unit() is not None:
            pass
        q.queue["sync"].append(((Token(q.sems["out"], q.count["out"]), Token(q.sems["c_out"], q.count["c_out"])),
                                lambda e: None, None, 0))

        block = ctx.enter_context(nc.Block())

        @block.sync
        def _(eng):
            q.run("sync", eng)

        @block.gpsimd
        def _(eng):
            q.run("gpsimd", eng)

        @block.scalar
        def _(eng):
            q.run("scalar", eng)

        @block.vector
        def _(eng):
            q.run("vector", eng)

        @block.tensor
        def _(eng):
            q.run("tensor", eng)




def lay_out(i):
    c = np.ascontiguousarray

    def chunks(w):
        *lead, k, n = w.shape
        w = w.reshape(*lead, k // P, P, n)
        return c(np.moveaxis(w, -2, 0))

    x, ctx = i["x"], i["ctx_1024"]
    rowsT = lambda a: c(a.transpose(0, 2, 1).reshape(ROWS, KD, P, L).transpose(0, 2, 1, 3))
    rows = lambda a: c(a.reshape(ROWS, KL, P, D).transpose(0, 2, 1, 3))
    xp = i["L0_attn_x_proj_w"]
    Bw, Cw, dtw = xp[:, R:R + S], xp[:, R + S:], xp[:, :R]
    lo, hi = Bw[:, :HALF], Bw[:, HALF:]
    wx = np.concatenate([lo, lo, lo, hi, hi, hi, Cw, dtw], axis=1)
    w_dt = np.concatenate([i["L0_attn_dt_proj_w"].transpose(0, 2, 1), i["L0_attn_dt_proj_b"][:, None, :]], axis=1)
    conv = np.concatenate([i["L0_attn_conv_w"], i["L0_attn_conv_b"][:, :, None]], axis=2)
    w1 = i["L0_ffn_w1"].transpose(0, 2, 1).reshape(E, KD, P, 2, HID // 2).transpose(0, 3, 2, 1, 4)
    w2 = i["L0_ffn_w2"].transpose(0, 2, 1).reshape(E, 2, KH // 2, P, D).transpose(0, 1, 3, 2, 4)
    w_exp = np.concatenate([w1.reshape(E, 2, P, HID), w2.reshape(E, 2, P, HID)], axis=3)
    att = np.stack([i[f"L0_xattn_W{k}"].T for k in "qkvo"])
    return {
        "xT": rowsT(x), "x": rows(x), "ctxT": rowsT(ctx),
        "w_in": chunks(i["L0_attn_in_proj_w"].transpose(0, 2, 1)),
        "conv": chunks(conv),
        "w_x": chunks(wx.transpose(0, 2, 1)),
        "w_dt": c(w_dt.transpose(1, 0, 2)),
        "A_log": chunks(i["L0_attn_A_log"]),
        "D_skip": c(i["L0_attn_D_skip"].reshape(LAYERS, KI, P).transpose(2, 0, 1)),
        "w_out": chunks(i["L0_attn_out_proj_w"].transpose(0, 2, 1)),
        "w_att": chunks(att),
        "b_att": c(np.stack([i["L0_xattn_bq"], i["L0_xattn_bv"]]).reshape(2, KD, P).transpose(2, 0, 1)),
        "bo": c(i["L0_xattn_bo"].reshape(1, D)),
        "w_gate": chunks(i["L0_ffn_gate_w"].T),
        "b1": c(i["L0_ffn_b1"].reshape(E, KH, P).transpose(2, 0, 1)),
        "b2": c(i["L0_ffn_b2"]),
        "w_exp": c(w_exp),
    }


def kernel(**inputs):
    import concourse.bacc as bacc
    from concourse.bass_utils import run_bass_kernel_spmd

    nc = bacc.Bacc("TRN2", target_bir_lowering=False, num_devices=1)
    arrays = {f"in_{n}": a for n, a in lay_out(inputs).items()}
    io = {n[3:]: nc.dram_tensor(n, a.shape, mybir.dt.from_np(a.dtype), kind="ExternalInput").ap()
          for n, a in arrays.items()}
    out = nc.dram_tensor("y", (ROWS, P, KL, D), F32, kind="ExternalOutput").ap()
    decoder_block(nc, io, out)
    r = run_bass_kernel_spmd(nc, [arrays], core_ids=[0])
    y = r.results[0]["y"]
    return np.ascontiguousarray(y.transpose(0, 2, 1, 3).reshape(ROWS, L, D))
```
